# Optimizing a Trainium2 kernel written in Bass

```python
import numpy as np
import jax
import jax.numpy as jnp

def _softmax(x, axis=-1):
    return jax.nn.softmax(x, axis=axis)

def _gelu(x):
    return jax.nn.gelu(x, approximate=True)

def _silu(x):
    return jax.nn.silu(x)

def _sigmoid(x):
    return jax.nn.sigmoid(x)

def _layernorm(x, axis=-1, eps=1e-05):
    m = jnp.mean(x, axis=axis, keepdims=True)
    v = jnp.var(x, axis=axis, keepdims=True)
    return (x - m) / jnp.sqrt(v + eps)

def _scatter_add(tgt, idx, src, axis=0):
    return tgt.at[idx].add(src)

def _segment_sum(src, seg, n):
    return jax.ops.segment_sum(src, seg, n)
kernel_name = 'mk_xattn_ffn_d1_seqx_r8_51f745'

def setup_inputs(seed: int=0):
    np.random.seed(seed)
    _w = jnp.asarray

    def _rec_inputs():
        import jax
        import jax.numpy as jnp
        _rk = jax.random.key(seed)
        x = -0.0003929 + 0.9999 * jax.random.normal(jax.random.fold_in(_rk, 1), (8, 128, 512), jnp.float32)
        _lenS = 128 - jax.random.randint(jax.random.fold_in(_rk, 7), (8,), 0, max(1, 128 // 4) + 1, jnp.int32)
        _lenS2 = 128 - jax.random.randint(jax.random.fold_in(_rk, 8), (8,), 0, max(1, 128 // 4) + 1, jnp.int32)
        _ctx_4096P = jax.random.normal(jax.random.fold_in(_rk, 11), (8, 16, 512), jnp.float32)
        _ctx_4096c = jax.random.dirichlet(jax.random.fold_in(_rk, 511), 0.3 * jnp.ones((16,), jnp.float32), (8, 128))
        _ctx_4096t = jnp.einsum('bsk,bkd->bsd', _ctx_4096c, _ctx_4096P)
        _ctx_4096t = _ctx_4096t * jax.lax.rsqrt(jnp.mean(jnp.square(_ctx_4096t)) + 1e-12) * 0.953939
        ctx_4096 = 2.81802e-05 + 1.00001 * (_ctx_4096t + 0.3 * jax.random.normal(jax.random.fold_in(_rk, 611), (8, 128, 512), jnp.float32))
        return (x, ctx_4096)
    x, ctx_4096 = _rec_inputs()

    def _L0_xattn_setup():
        import jax, jax.numpy as jnp
        import numpy as np
        HID = 512
        NHEAD = 32
        NKV = 8
        HDIM = 128
        G = NHEAD // NKV
        key = jax.random.key(seed)
        ks = jax.random.split(key, 6)
        s = 0.02
        B, L = (2, 256)
        return {'query': jax.random.normal(ks[0], (B, L, HID), jnp.float32), 'kv': jax.random.normal(ks[1], (B, L, HID), jnp.float32), 'Wq': jax.random.normal(ks[2], (HID, NHEAD * HDIM), jnp.float32) * s, 'bq': jnp.zeros((NHEAD * HDIM,), jnp.float32), 'Wkv': jax.random.normal(ks[3], (HID, 2 * NKV * HDIM), jnp.float32) * s, 'bkv': jnp.zeros((2 * NKV * HDIM,), jnp.float32), 'Wo': jax.random.normal(ks[4], (NHEAD * HDIM, HID), jnp.float32) * s, 'bo': jnp.zeros((HID,), jnp.float32)}
    _L0_xattn_all = _L0_xattn_setup()
    _L0_xattn_in = {k: v for k, v in _L0_xattn_all.items() if k in ('Wq', 'bq', 'Wkv', 'bkv', 'Wo', 'bo')}
    del _L0_xattn_all

    def _L0_ffn_setup():
        import jax, jax.numpy as jnp
        import numpy as np
        SCALING = 16.0 / 8.0
        GAMMA = 1.0
        EPS = 1e-12
        key = jax.random.key(seed)
        ks = jax.random.split(key, 8)
        B, T, H, O = (4, 256, 512, 512)
        E_tot, E_act, r = (16, 4, 8)
        return {'x': jax.random.normal(ks[0], (B, T, H), jnp.float32), 'W_base': jax.random.normal(ks[1], (O, H), jnp.float32) * 0.02, 'b_base': jax.random.normal(ks[2], (O,), jnp.float32) * 0.02, 'lora_A': jax.random.normal(ks[3], (E_tot, r, H), jnp.float32) * 0.02, 'lora_B': jax.random.normal(ks[4], (E_tot, O, r), jnp.float32) * 0.02, 'router_W': jax.random.normal(ks[5], (E_tot, H), jnp.float32) * 0.02, 'router_b': jax.random.normal(ks[6], (E_tot,), jnp.float32) * 0.02, 'domain_prior': jax.random.uniform(ks[7], (E_tot,), jnp.float32), 'active': jnp.arange(E_act, dtype=jnp.int32)}
    _L0_ffn_all = _L0_ffn_setup()
    _L0_ffn_in = {k: v for k, v in _L0_ffn_all.items() if k in ('W_base', 'b_base', 'lora_A', 'lora_B', 'router_W', 'router_b', 'domain_prior', 'active')}
    del _L0_ffn_all
    return {'x': x, 'ctx_4096': ctx_4096, 'L0_xattn_Wq': _L0_xattn_in['Wq'], 'L0_xattn_bq': _L0_xattn_in['bq'], 'L0_xattn_Wkv': _L0_xattn_in['Wkv'], 'L0_xattn_bkv': _L0_xattn_in['bkv'], 'L0_xattn_Wo': _L0_xattn_in['Wo'], 'L0_xattn_bo': _L0_xattn_in['bo'], 'L0_ffn_W_base': _L0_ffn_in['W_base'], 'L0_ffn_b_base': _L0_ffn_in['b_base'], 'L0_ffn_lora_A': _L0_ffn_in['lora_A'], 'L0_ffn_lora_B': _L0_ffn_in['lora_B'], 'L0_ffn_router_W': _L0_ffn_in['router_W'], 'L0_ffn_router_b': _L0_ffn_in['router_b'], 'L0_ffn_domain_prior': _L0_ffn_in['domain_prior'], 'L0_ffn_active': _L0_ffn_in['active']}

def reference(x, ctx_4096, L0_xattn_Wq, L0_xattn_bq, L0_xattn_Wkv, L0_xattn_bkv, L0_xattn_Wo, L0_xattn_bo, L0_ffn_W_base, L0_ffn_b_base, L0_ffn_lora_A, L0_ffn_lora_B, L0_ffn_router_W, L0_ffn_router_b, L0_ffn_domain_prior, L0_ffn_active):
    import jax
    import jax.numpy as jnp

    def _L0_xattn_ref(query, kv, Wq, bq, Wkv, bkv, Wo, bo):
        import jax, jax.numpy as jnp
        import numpy as np
        HID = 512
        NHEAD = 32
        NKV = 8
        HDIM = 128
        G = NHEAD // NKV
        B, L, _ = query.shape
        Lk = kv.shape[1]
        scale = jnp.asarray(1.0 / np.sqrt(HDIM), query.dtype)
        q = (query @ Wq + bq).reshape(B, L, NKV, G, HDIM)
        k_, v_ = jnp.split(kv @ Wkv + bkv, 2, axis=-1)
        k = k_.reshape(B, Lk, NKV, HDIM)
        v = v_.reshape(B, Lk, NKV, HDIM)
        scores = jnp.einsum('blkgd,bmkd->bkglm', q, k) * scale
        attn = jax.nn.softmax(scores, axis=-1)
        o = jnp.einsum('bkglm,bmkd->blkgd', attn, v).reshape(B, L, NHEAD * HDIM)
        return o @ Wo + bo

    def _L0_ffn_ref(x, W_base, b_base, lora_A, lora_B, router_W, router_b, domain_prior, active):
        import jax, jax.numpy as jnp
        import numpy as np
        SCALING = 16.0 / 8.0
        GAMMA = 1.0
        EPS = 1e-12
        y = jnp.einsum('bth,oh->bto', x, W_base) + b_base
        A = lora_A[active]
        Bm = lora_B[active]
        z = jnp.einsum('bth,erh->bter', x, A)
        contribs = jnp.einsum('bter,eor->bteo', z, Bm) * SCALING
        logits = jnp.einsum('bth,eh->bte', x, router_W) + router_b
        logits = logits[..., active]
        prior = domain_prior[active]
        alpha = jax.nn.softmax(jnp.log(prior + EPS) + logits / GAMMA, axis=-1)
        return y + jnp.einsum('bteo,bte->bto', contribs, alpha)
    x = x + _L0_xattn_ref(_layernorm(x, axis=-1), ctx_4096, L0_xattn_Wq, L0_xattn_bq, L0_xattn_Wkv, L0_xattn_bkv, L0_xattn_Wo, L0_xattn_bo)
    x = x + _L0_ffn_ref(_layernorm(x, axis=-1), L0_ffn_W_base, L0_ffn_b_base, L0_ffn_lora_A, L0_ffn_lora_B, L0_ffn_router_W, L0_ffn_router_b, L0_ffn_domain_prior, L0_ffn_active)
    return x

_drawn_inputs = setup_inputs


def setup_inputs(seed=0):
    import zlib

    import numpy as np

    out = dict(_drawn_inputs(seed))
    spreads = {'L0_xattn_bq': (0.0, 0.8), 'L0_xattn_bkv': (0.0, 0.1), 'L0_xattn_bo': (0.0, 0.1)}
    factors = {'L0_xattn_Wq': 2.784,
     'L0_ffn_b_base': 3.373,
     'L0_ffn_router_W': 7.11,
     'L0_ffn_router_b': 200.0,
     'L0_ffn_domain_prior': 200.0}
    for name, (base, spread) in spreads.items():
        noise = np.random.default_rng([zlib.crc32(name.encode()), seed]).standard_normal(out[name].shape)
        drawn = base * np.exp(spread * noise) if base else spread * noise
        out[name] = jnp.asarray(drawn.astype(out[name].dtype))
    for name, factor in factors.items():
        out[name] = (out[name] * factor).astype(out[name].dtype)
    return out
```

```python
from contextlib import ExitStack

import concourse.bass as bass
from concourse import mybir

F32 = mybir.dt.float32
F32R = mybir.dt.float32r
I32 = mybir.dt.int32
ALU = mybir.AluOpType
ACT = mybir.ActivationFunctionType
AX_X = mybir.AxisListType.X

P = 128
B = 8
HID = 512
C = HID // P
G = 8
H = 4
UNITS = G * B
PAIRS = G // 2
PU = 2 * B
HALF = B // 2 * P
E_TOT, E_ACT, RANK = 16, 4, 8
ER, JR = E_TOT * RANK, E_ACT * RANK
SCALE = float(P) ** -0.5
EPS = 1e-5
PRIOR_EPS = 1e-12
LORA_SCALING = 16.0 / 8.0

PROLOGUE_JOBS = ([("k", 0)] + [("v", b) for b in range(7)] + [("q", j) for j in range(5)]
                 + [("v", 7), ("q", 5)])
KEY_SLOTS = {0: 1, 3: 2, 8: 3, 11: 4}
VALUE_SLOTS = {7 + b: b for b in range(B)}


def slot_jobs(w, last):
    jobs = []
    if not (last and w + 6 >= PU):
        jobs.append(("q", w + 6))
    if w in KEY_SLOTS and not (last and KEY_SLOTS[w] == 4):
        jobs.append(("k", KEY_SLOTS[w]))
    if w in VALUE_SLOTS and not last:
        jobs.append(("v", B + VALUE_SLOTS[w]))
    if last and w == 1:
        jobs.append(("a", 0))
    if last and w == 5:
        jobs.append(("b", 0))
    return jobs


PER_PAIR = {"q": PU, "k": 4, "v": B, "a": 0, "b": 0}


def job_plan(last):
    order = [(None, k, i) for k, i in PROLOGUE_JOBS]
    body = [(w, k, i) for w in range(PU) for k, i in slot_jobs(w, last)]
    plan, n = {}, len(order)
    before = [(k, i) for _, k, i in order[-2:]]
    for w, k, i in body:
        plan[(w, k, i)] = (n % 2, before[0])
        before = [before[1], (k, i)]
        n += 1
    return plan


def check_plan():
    body = [(k, i) for w in range(PU) for k, i in slot_jobs(w, False)]
    assert len(body) % 2 == 0
    assert [(k, i - PER_PAIR[k]) for k, i in body[-2:]] == PROLOGUE_JOBS[-2:]


def build(nc, x, ctx_t, wq, wk, wv, wo, bq, bk, bv, bo, w_base, b_base, lora_a, lora_b,
          router_w, router_b, prior, active, out):
    check_plan()
    stack = ExitStack()
    with stack:
        def sb(name, shape, dt=F32):
            return stack.enter_context(nc.sbuf_tensor(name, shape, dt))

        def ps(name, shape):
            return stack.enter_context(nc.psum_tensor(name, shape, F32))

        def sem(name):
            return stack.enter_context(nc.semaphore(name))

        xn_hi = sb("xn_hi", [P, C, B * P], F32R)
        xn_lo = sb("xn_lo", [P, C, B * P], F32R)
        ctx_hi = sb("ctx_hi", [P, C, B * P], F32R)
        ctx_lo = sb("ctx_lo", [P, C, B * P], F32R)
        wq_hi = sb("wq_hi", [P, H, C, P], F32R)
        wq_lo = sb("wq_lo", [P, H, C, P], F32R)
        wo_hi = sb("wo_hi", [P, H, HID], F32R)
        wo_lo = sb("wo_lo", [P, H, HID], F32R)
        wk_hi = sb("wk_hi", [P, C, P], F32R)
        wk_lo = sb("wk_lo", [P, C, P], F32R)
        wv_hi = sb("wv_hi", [P, C, 2 * P], F32R)
        wv_lo = sb("wv_lo", [P, C, 2 * P], F32R)
        raw_q = sb("raw_q", [P, 2, C, P])
        raw_o = sb("raw_o", [P, H, HID])
        raw_k = sb("raw_k", [P, C, P])
        raw_v = sb("raw_v", [P, C, 2 * P])
        k_t = sb("k_t", [P, B * P])
        v_hi = sb("v_hi", [P, B, 2 * P], F32R)
        v_lo = sb("v_lo", [P, B, 2 * P], F32R)
        q_t = sb("q_t", [P, 8, HALF])
        prob = sb("prob", [P, 2, H, P])
        pt_hi = sb("pt_hi", [P, H * P], F32R)
        pt_lo = sb("pt_lo", [P, H * P], F32R)
        ot_hi = sb("ot_hi", [P, 2, H * P], F32R)
        ot_lo = sb("ot_lo", [P, 2, H * P], F32R)
        y = sb("y", [P, B, HID])
        norm_x = sb("norm_x", [P, 2, HID])
        x2_t = sb("x2_t", [P, C, P])
        ident = sb("ident", [P, P])
        bias_q = sb("bias_q", [P, G * H])
        bias_k = sb("bias_k", [P, G])
        bias_v = sb("bias_v", [P, G])
        pair_q = sb("pair_q", [P, 3 * H])
        pair_k = sb("pair_k", [P, 3])
        pair_v = sb("pair_v", [P, 3])
        neg_max = sb("neg_max", [P, 2, H])
        exp_sum = sb("exp_sum", [P, 2, H])
        inv_sum = sb("inv_sum", [P, 2, H])
        stats = sb("stats", [P, B, 6])
        mean_var = sb("mean_var", [P, B, 2])
        var_eps = sb("var_eps", [P, B])
        rstd = sb("rstd", [P, B])
        minus_half = sb("minus_half", [P, B])
        prior_eps = sb("prior_eps", [P, 1])
        ones = sb("ones", [P, P])
        act_i = sb("act_i", [P, E_ACT], I32)
        act_f = sb("act_f", [P, E_ACT])
        act_neg = sb("act_neg", [P, E_ACT])
        iota_i = sb("iota_i", [P, RANK], I32)
        iota_f = sb("iota_f", [P, RANK])
        sel_r = sb("sel_r", [P, E_ACT, RANK])
        sel_e = sb("sel_e", [E_TOT, E_ACT])
        prior_in = sb("prior_in", [E_TOT, 2])
        prior_rows = sb("prior_rows", [E_TOT, 2, P])
        log_prior = sb("log_prior", [P, E_ACT])
        gate_bias = sb("gate_bias", [P, E_ACT])
        az = sb("az", [P, C, JR + E_ACT])
        b_sel = sb("b_sel", [JR + 1, HID])
        gates = sb("gates", [P, 4, E_ACT])
        g_max, g_sum, g_inv = (sb(n, [P, 1]) for n in ("g_max", "g_sum", "g_inv"))
        za = sb("za", [P, E_ACT, RANK])
        za_t = sb("za_t", [JR + 1, P])
        bo_all = x2_t[:, :, :].rearrange("p c n -> p (c n)")
        ctx_raw = q_t[:, :, :].rearrange("p a n -> p (a n)").rearrange("p (s c n) -> p s c n", s=2, c=C)
        lb_raw = norm_x[:, 0, :]
        la_raw = raw_v[:, 0:2, :].rearrange("p c n -> p (c n)")
        rw_raw = raw_v[0:E_TOT, 2:4, :].rearrange("p c n -> p (c n)")
        x2_hi = [xn_hi[:, :, i * P:(i + 1) * P] for i in range(2)]
        x2_lo = [xn_lo[:, :, i * P:(i + 1) * P] for i in range(2)]

        score_ps = ps("score_ps", [P, 2, H * P])
        pt_ps = ps("pt_ps", [P, H * P])
        att_ps = ps("att_ps", [P, H * P])
        job_ps = ps("job_ps", [P, 2, HID])
        out_ps = ps("out_ps", [P, 2, HID])

        small_in, ffn_in, bo_in, base_in = (sem(n) for n in ("small_in", "ffn_in", "bo_in", "base_in"))
        ctx_in = [sem(f"ctx_in{i}") for i in range(2)]
        x_in = [sem(f"x_in{i}") for i in range(2)]
        rawq_in = [sem(f"rawq_in{i}") for i in range(2)]
        rawo_in = [sem(f"rawo_in{i}") for i in range(H)]
        rawk_in, rawv_in = sem("rawk_in"), sem("rawv_in")
        ctx_hi_done, ctx_lo_done = sem("ctx_hi_done"), sem("ctx_lo_done")
        hi_done = {k: sem(f"w{k}_hi_done") for k in "qokv"}
        lo_done = {k: sem(f"w{k}_lo_done") for k in "qokv"}
        job_done = {k: sem(f"job_{k}_done") for k in "qkvab"}
        q_stored, k_stored = sem("q_stored"), sem("k_stored")
        vhi_stored, vlo_stored = sem("vhi_stored"), sem("vlo_stored")
        az_stored, bsel_stored = sem("az_stored"), sem("bsel_stored")
        scored, maxed, exped, inverted, normed = (sem(n) for n in (
            "scored", "maxed", "exped", "inverted", "normed"))
        transposed, pthi_stored, ptlo_stored = sem("transposed"), sem("pthi_stored"), sem("ptlo_stored")
        attended, othi_stored, otlo_stored = sem("attended"), sem("othi_stored"), sem("otlo_stored")
        projected, y_added = sem("projected"), sem("y_added")
        biases_picked = sem("biases_picked")
        const_done, ident_done, sel_step, bias_done = (sem(n) for n in (
            "const_done", "ident_done", "sel_step", "bias_done"))
        prior_picked, prior_logged, gate_bias_done = (sem(n) for n in (
            "prior_picked", "prior_logged", "gate_bias_done"))
        stats_done, aggr_done, eps_added, rstd_done, rows_normed = (sem(n) for n in (
            "stats_done", "aggr_done", "eps_added", "rstd_done", "rows_normed"))
        rows_turned, xhi_stored, xlo_stored = sem("rows_turned"), sem("xhi_stored"), sem("xlo_stored")
        x2t_stored, x2hi_stored, x2lo_stored = sem("x2t_stored"), sem("x2hi_stored"), sem("x2lo_stored")
        lora_in_done, gate_step, gate_exped = sem("lora_in_done"), sem("gate_step"), sem("gate_exped")
        za_turned, zat_stored = sem("za_turned"), sem("zat_stored")
        ffn_done, out_added, out_stored = sem("ffn_done"), sem("out_added"), sem("out_stored")

        block = stack.enter_context(nc.Block())

        def stored(kind, p, index):
            s = {"q": q_stored, "k": k_stored, "v": vlo_stored, "a": az_stored, "b": bsel_stored}
            return s[kind], PER_PAIR[kind] * p + index + 1

        def over_pairs(eng, body):
            with eng.Fori(0, PAIRS - 1, 1) as p:
                body(p, False)
            body(PAIRS - 1, True)

        def ffn_batches(u):
            turn, mix = u - (UNITS - B + 1), u - (UNITS - B + 2)
            return (turn if 0 <= turn < B else None), (mix if 0 <= mix < B else None)

        ENDING = range(UNITS, UNITS + 2)

        @block.sync
        def _(sp):
            def load_q(p, n):
                s = n % 2
                sp.dma_start(raw_q[:, s, :, :], wq[PU // 2 * p + n, :, :, :]).then_inc(rawq_in[s], 16)

            for half in range(2):
                if half == 0:
                    sp.dma_start(ctx_raw[:, 0, :, :], ctx_t[:, :, 0:HALF]).then_inc(ctx_in[0], 16)
                    sp.dma_start(raw_k[:, :, :], wk[0, :, :, :]).then_inc(rawk_in, 16)
                    sp.dma_start(raw_v[:, :, :], wv[0, :, :, :]).then_inc(rawv_in, 16)
                    sp.dma_start(y[:, 0:B // 2, :], x[:, 0:B // 2, :]).then_inc(x_in[0], 16)
                else:
                    sp.dma_start(ctx_raw[:, 1, :, :], ctx_t[:, :, HALF:2 * HALF]).then_inc(ctx_in[1], 16)
                    sp.dma_start(y[:, B // 2:B, :], x[:, B // 2:B, :]).then_inc(x_in[1], 16)
            for n in range(2):
                load_q(0, n)
            for n in range(2, H):
                sp.wait_ge(lo_done["q"], n - 1)
                load_q(0, n)
            sp.dma_start(bo_all, bo.to_broadcast([P, HID])).then_inc(bo_in, 16)
            for h in range(H):
                sp.dma_start(raw_o[:, h, :], wo[h, :, :]).then_inc(rawo_in[h], 16)

            def loads(p, last):
                for odd in range(2):
                    if not (last and odd):
                        for h in range(H):
                            n = H * (odd + 1) + h
                            sp.wait_ge(lo_done["q"], 8 * p + n - 1)
                            load_q(p, n)
                            if h == 1:
                                sp.wait_ge(lo_done["k"], 2 * p + odd + 1)
                                sp.dma_start(raw_k[:, :, :], wk[2 * p + odd + 1, :, :, :]).then_inc(rawk_in, 16)
                        if odd == 0 and not last:
                            sp.wait_ge(lo_done["v"], p + 1)
                            sp.dma_start(raw_v[:, :, :], wv[p + 1, :, :, :]).then_inc(rawv_in, 16)
                    for h in range(H):
                        sp.wait_ge(lo_done["o"], 8 * p + H * odd + h + 1)
                        if last and odd:
                            sp.dma_start(raw_o[:, h, :], w_base[h, :, :]).then_inc(rawo_in[h], 16)
                        else:
                            sp.dma_start(raw_o[:, h, :], wo[8 * p + H * (odd + 1) + h, :, :]).then_inc(rawo_in[h], 16)
                    if last and odd == 0:
                        sp.wait_ge(rows_turned, B)
                        sp.dma_start(lb_raw, lora_b).then_inc(ffn_in, 16)
                        sp.dma_start(la_raw, lora_a).then_inc(ffn_in, 16)
                        sp.dma_start(rw_raw, router_w).then_inc(ffn_in, 16)
                        sp.dma_start(b_sel[JR:JR + 1, :], b_base).then_inc(ffn_in, 16)

            over_pairs(sp, loads)
            for b in range(B):
                sp.wait_ge(out_added, b + 1)
                sp.dma_start(out[b, :, :], y[:, b, :]).then_inc(out_stored, 16)
            sp.wait_ge(out_stored, 16 * B)

        @block.gpsimd
        def _(pool):
            nc.gpsimd.memset(ident[:, :], 0.0).then_inc(const_done, 1)
            nc.gpsimd.memset(ones[:, :], 1.0).then_inc(const_done, 1)
            nc.gpsimd.memset(minus_half[:, :], -0.5).then_inc(const_done, 1)
            nc.gpsimd.memset(prior_eps[:, :], PRIOR_EPS).then_inc(const_done, 1)
            pool.wait_ge(const_done, 4)
            nc.gpsimd.memset(za_t[JR:JR + 1, :], 1.0).then_inc(const_done, 1)
            pool.wait_ge(const_done, 5)
            nc.gpsimd.iota(iota_i[:, :], pattern=[[1, RANK]], base=0, channel_multiplier=-1).then_inc(const_done, 1)
            pool.wait_ge(const_done, 6)
            nc.gpsimd.affine_select(out=ident[:, :], in_=ident[:, :], compare_op=ALU.not_equal, fill=1.0,
                                    base=0, pattern=[[-1, P]], channel_multiplier=1).then_inc(ident_done, 1)

            def low(kind, p, n, dst, raw, hi):
                pool.wait_ge(hi_done[kind], p + n + 1)
                nc.gpsimd.tensor_tensor(dst, raw, hi.bitcast(F32), ALU.subtract).then_inc(lo_done[kind], 1)

            def low_q(p, n):
                h = n % H
                low("q", 8 * p, n, wq_lo[:, h, :, :], raw_q[:, n % 2, :, :], wq_hi[:, h, :, :])

            def low_o(p, n):
                h = n % H
                low("o", 8 * p, n, wo_lo[:, h, :], raw_o[:, h, :], wo_hi[:, h, :])

            def low_k(p, n):
                low("k", 2 * p, n, wk_lo[:, :, :], raw_k[:, :, :], wk_hi[:, :, :])

            def low_v(p, n):
                low("v", p, n, wv_lo[:, :, :], raw_v[:, :, :], wv_hi[:, :, :])

            def power(first, count):
                nc.gpsimd.tensor_tensor(rstd[:, first:first + count], var_eps[:, first:first + count],
                                        minus_half[:, 0:count], ALU.pow).then_inc(rstd_done, 1)

            low_k(0, 0)
            low_v(0, 0)
            for half in range(2):
                pool.wait_ge(eps_added, half + 1)
                power(half * B // 2, B // 2)
            for n in range(H):
                low_q(0, n)
            pool.wait_ge(bo_in, 16)
            for b in range(B):
                pool.wait_ge(rows_normed, b + 1)
                nc.gpsimd.tensor_tensor(y[:, b, :], y[:, b, :], bo_all, ALU.add).then_inc(y_added, 1)
            for n in range(H):
                low_o(0, n)

            def lows(p, last):
                for w in range(PU):
                    odd, wg = divmod(w, B)
                    if wg < H and not (last and odd):
                        low_q(p, H * (odd + 1) + wg)
                        if wg == 1:
                            low_k(p, odd + 1)
                    if w == 4 and not last:
                        low_v(p, 1)
                    if wg == 7 and not (last and odd):
                        for h in range(H):
                            low_o(p, H * (odd + 1) + h)
                    if last and odd:
                        if wg == 1:
                            for c in range(C):
                                pool.wait_ge(hi_done["o"], H * G + c + 1)
                                nc.gpsimd.tensor_tensor(ctx_lo[:, c, 0:HID], raw_o[:, c, :],
                                                        ctx_hi[:, c, 0:HID].bitcast(F32),
                                                        ALU.subtract).then_inc(lo_done["o"], 1)
                        pool.wait_ge(eps_added, 2 + wg + 1)
                        power(wg, 1)

            over_pairs(pool, lows)

        @block.scalar
        def _(act):
            act.dma_start(act_i[:, :], active.to_broadcast([P, E_ACT])).then_inc(small_in, 16)
            act.dma_start(prior_in[:, 0:1], prior).then_inc(small_in, 16)
            act.dma_start(prior_in[:, 1:2], router_b).then_inc(small_in, 16)
            act.dma_start(bias_q[:, :], bq).then_inc(small_in, 16)
            act.dma_start(bias_k[:, :], bk).then_inc(small_in, 16)
            act.dma_start(bias_v[:, :], bv).then_inc(small_in, 16)
            act.wait_ge(const_done, 6)
            act.wait_ge(prior_picked, 1)
            nc.scalar.activation(log_prior[:, :], out_ps[:, 0, 0:E_ACT], ACT.Ln,
                                 bias=prior_eps[:, 0:1]).then_inc(prior_logged, 1)

            def high(kind, base, n, dst, raw):
                nc.scalar.activation(dst, raw, ACT.Copy).then_inc(hi_done[kind], 1)

            def high_q(p, n, first=False):
                h = n % H
                act.wait_ge(rawq_in[n % 2], 16 * (4 * p + n // 2 + 1))
                if not first:
                    act.wait_ge(job_done["q"], PU * p + B * (n // H - 1) + H + h + 1)
                high("q", 8 * p, n, wq_hi[:, h, :, :], raw_q[:, n % 2, :, :])

            def high_o(p, n, first=False):
                h = n % H
                act.wait_ge(rawo_in[h], 16 * (2 * p + n // H + 1))
                if not first:
                    act.wait_ge(projected, H * PU * p + H * B * (n // H) - H + h + 1)
                high("o", 8 * p, n, wo_hi[:, h, :], raw_o[:, h, :])

            def high_k(p, n, first=False):
                act.wait_ge(rawk_in, 16 * (2 * p + n + 1))
                if not first:
                    act.wait_ge(job_done["k"], 4 * p + 2 * n)
                high("k", 2 * p, n, wk_hi[:, :, :], raw_k[:, :, :])

            def high_v(p, n, first=False):
                act.wait_ge(rawv_in, 16 * (p + n + 1))
                if not first:
                    act.wait_ge(job_done["v"], B * (p + n))
                high("v", p, n, wv_hi[:, :, :], raw_v[:, :, :])

            def pick_biases(p, groups, picked):
                nc.scalar.copy(pair_q[:, 0:H * groups], bias_q[:, bass.ds(8 * p, H * groups)]).then_inc(biases_picked, 1)
                nc.scalar.copy(pair_k[:, 0:groups], bias_k[:, bass.ds(2 * p, groups)]).then_inc(biases_picked, 1)
                nc.scalar.copy(pair_v[:, 0:groups], bias_v[:, bass.ds(2 * p, groups)]).then_inc(biases_picked, 1)
                act.wait_ge(biases_picked, picked)

            def store_q(bank, p, n):
                act.wait_ge(job_done["q"], PU * p + n + 1)
                head = H * (n // B) + n % H
                nc.scalar.activation(q_t[:, n % 8, :], job_ps[:, bank, :], ACT.Identity,
                                     bias=pair_q[:, head:head + 1], scale=SCALE).then_inc(q_stored, 1)

            def store_k(bank, p, n):
                half = n % 2
                act.wait_ge(job_done["k"], 4 * p + n + 1)
                nc.scalar.activation(k_t[:, half * HALF:(half + 1) * HALF], job_ps[:, bank, :], ACT.Identity,
                                     bias=pair_k[:, n // 2:n // 2 + 1]).then_inc(k_stored, 1)

            def store_v(bank, p, n):
                act.wait_ge(job_done["v"], B * p + n + 1)
                nc.scalar.activation(v_hi[:, n % B, :], job_ps[:, bank, 0:2 * P], ACT.Copy).then_inc(vhi_stored, 1)

            def store_az(bank):
                act.wait_ge(job_done["a"], 1)
                nc.scalar.activation(az[:, :, :], job_ps[:, bank, 0:C * (JR + E_ACT)].rearrange(
                    "p (c n) -> p c n", c=C), ACT.Copy).then_inc(az_stored, 1)

            def store_bsel(bank):
                act.wait_ge(job_done["b"], 1)
                nc.scalar.activation(b_sel[0:JR, :], job_ps[0:JR, bank, :], ACT.Copy).then_inc(bsel_stored, 1)

            def exps(u, par):
                act.wait_ge(maxed, u + 1)
                for h in range(H):
                    last = nc.scalar.activation(prob[:, par, h, :], score_ps[:, par, h * P:(h + 1) * P], ACT.Exp,
                                                bias=neg_max[:, par, h:h + 1],
                                                accum_out=exp_sum[:, par, h:h + 1])
                last.then_inc(exped, 1)

            def store_pt(t):
                act.wait_ge(transposed, t + 1)
                nc.scalar.activation(pt_hi[:, :], pt_ps[:, :], ACT.Copy).then_inc(pthi_stored, 1)

            def store_ot(t, par, group):
                act.wait_ge(attended, t + 1)
                nc.scalar.activation(ot_hi[:, par, :], att_ps[:, :], ACT.Identity,
                                     bias=pair_v[:, group:group + 1]).then_inc(othi_stored, 1)

            def store_x(b):
                act.wait_ge(rows_turned, b + 1)
                nc.scalar.activation(xn_hi[:, :, b * P:(b + 1) * P],
                                     out_ps[:, b % 2, :].rearrange("p (c n) -> p c n", c=C),
                                     ACT.Copy).then_inc(xhi_stored, 1)

            def split_ctx(half):
                act.wait_ge(ctx_in[half], 16)
                for c2 in range(2):
                    nc.scalar.activation(ctx_hi[:, 2 * c2:2 * c2 + 2, half * HALF:(half + 1) * HALF],
                                         ctx_raw[:, half, 2 * c2:2 * c2 + 2, :], ACT.Copy).then_inc(ctx_hi_done, 1)

            plan = {}
            for n, (kind, index) in enumerate(PROLOGUE_JOBS):
                plan[(kind, index)] = n % 2
            split_ctx(0)
            high_k(0, 0, True)
            high_v(0, 0, True)
            act.wait_ge(bias_done, 2)
            pick_biases(0, 3, 3)
            store_k(plan[("k", 0)], 0, 0)
            for b in range(4):
                store_v(plan[("v", b)], 0, b)
                if b == 1:
                    split_ctx(1)
            for b in range(4):
                store_x(b)
            for b in range(4, 7):
                store_v(plan[("v", b)], 0, b)
                if b < 6:
                    high_q(0, b - 4, True)
            high_q(0, 2, True)
            high_q(0, 3, True)
            for j in range(4):
                store_q(plan[("q", j)], 0, j)
            for b in range(4, 8):
                store_x(b)
            exps(0, 0)
            for h in range(H):
                high_o(0, h, True)
            store_q(plan[("q", 4)], 0, 4)
            exps(1, 1)
            store_v(plan[("v", 7)], 0, 7)
            store_pt(0)
            store_q(plan[("q", 5)], 0, 5)
            store_ot(0, 0, 0)

            def turn_x2(b):
                act.wait_ge(rows_turned, B + b + 1)
                src = job_ps[:, 0, :].rearrange("p (c n) -> p c n", c=C)
                nc.scalar.activation(x2_t[:, :, :], src, ACT.Copy).then_inc(x2t_stored, 1)
                nc.scalar.activation(x2_hi[b % 2], src, ACT.Copy).then_inc(x2hi_stored, 1)

            def gate_exp(b):
                act.wait_ge(gate_step, 5 * b + 2)
                nc.scalar.activation(gates[:, 1, :], gates[:, 0, :], ACT.Exp, bias=g_max[:, 0:1],
                                     accum_out=g_sum[:, 0:1]).then_inc(gate_exped, 1)

            def store_zat(b):
                act.wait_ge(za_turned, b + 1)
                nc.scalar.activation(za_t[0:JR, :], job_ps[0:JR, 0, 0:P], ACT.Copy).then_inc(zat_stored, 1)

            def body(p, last):
                jobs = job_plan(last)
                act.wait_ge(q_stored, PU * p + 6)
                act.wait_ge(k_stored, 4 * p + 1)
                act.wait_ge(othi_stored, PU * p + 1)
                pick_biases(p, 2 if last else 3, 3 * p + 6)
                for w in range(PU + (len(ENDING) if last else 0)):
                    u = PU * p + w
                    odd, wg = divmod(w, B)
                    turn, mix = ffn_batches(u) if last else (None, None)
                    if mix is not None:
                        gate_exp(mix)
                    if not (last and w + 1 >= PU):
                        store_pt(u + 1)
                    if not (last and w + 2 >= PU):
                        exps(u + 2, w % 2)
                    if mix is not None:
                        store_zat(mix)
                    if wg < H and not (last and odd):
                        high_q(p, H * (odd + 1) + wg)
                        if wg == 1:
                            high_k(p, odd + 1)
                    if w == 4 and not last:
                        high_v(p, 1)
                    mine = [(k, i) for k, i in (slot_jobs(w, last) if w < PU else [])]
                    for k, i in mine:
                        if k == "q":
                            store_q(jobs[(w, k, i)][0], p, i)
                    if not (last and w + 1 >= PU):
                        store_ot(u + 1, (w + 1) % 2, (w + 1) // B)
                    if turn is not None:
                        turn_x2(turn)
                    for k, i in mine:
                        if k == "k":
                            store_k(jobs[(w, k, i)][0], p, i)
                        if k == "v":
                            store_v(jobs[(w, k, i)][0], p, i)
                        if k == "a":
                            store_az(jobs[(w, k, i)][0])
                        if k == "b":
                            store_bsel(jobs[(w, k, i)][0])
                    if wg == 7 and w < PU and not (last and odd):
                        for h in range(H):
                            high_o(p, H * (odd + 1) + h)
                    if last and w == B:
                        act.wait_ge(job_done["k"], 2 * G)
                        act.wait_ge(job_done["v"], PAIRS * B)
                        for c in range(C):
                            act.wait_ge(rawo_in[c], 16 * (G + 1))
                            nc.scalar.activation(ctx_hi[:, c, 0:HID], raw_o[:, c, :],
                                                 ACT.Copy).then_inc(hi_done["o"], 1)

            over_pairs(act, body)

        @block.vector
        def _(dve):
            dve.wait_ge(small_in, 6 * 16)
            nc.vector.tensor_copy(act_f[:, :], act_i[:, :]).then_inc(sel_step, 1)
            nc.vector.tensor_scalar(bias_q[:, :], bias_q[:, :], SCALE, None, ALU.mult).then_inc(bias_done, 1)
            dve.wait_ge(const_done, 6)
            nc.vector.tensor_copy(iota_f[:, :], iota_i[:, :]).then_inc(bias_done, 1)
            for i in range(2):
                nc.vector.tensor_scalar(prior_rows[:, i, :], ones[0:E_TOT, :], prior_in[:, i:i + 1], None,
                                        ALU.mult).then_inc(sel_step, 1)
            dve.wait_ge(sel_step, 3)
            nc.vector.tensor_scalar(act_neg[:, :], act_f[:, :], 0.0, float(E_TOT), ALU.is_lt, ALU.mult).then_inc(sel_step, 1)
            dve.wait_ge(sel_step, 4)
            nc.vector.tensor_tensor(act_f[:, :], act_f[:, :], act_neg[:, :], ALU.add).then_inc(sel_step, 1)
            dve.wait_ge(sel_step, 5)
            nc.vector.tensor_scalar(act_f[:, :], act_f[:, :], float(E_TOT - 1), 0.0, ALU.min, ALU.max).then_inc(sel_step, 1)
            dve.wait_ge(sel_step, 6)
            dve.wait_ge(bias_done, 2)
            nc.vector.tensor_scalar(sel_e[:, :], act_f[0:E_TOT, :], iota_f[0:E_TOT, 0:1], 0.0, ALU.add,
                                    ALU.is_equal).then_inc(sel_step, 1)
            nc.vector.scalar_tensor_tensor(
                sel_r[:, :, :], act_f[:, :].unsqueeze(2).to_broadcast([P, E_ACT, RANK]), float(RANK),
                iota_f[:, :].unsqueeze(1).to_broadcast([P, E_ACT, RANK]), ALU.mult, ALU.add).then_inc(sel_step, 1)
            dve.wait_ge(sel_step, 8)
            nc.vector.tensor_scalar(sel_r[:, :, :], sel_r[:, :, :], 0.0, None, ALU.is_equal).then_inc(sel_step, 1)

            def ctx_low(half):
                for c2 in range(2):
                    dve.wait_ge(ctx_hi_done, 2 * half + c2 + 1)
                    part = slice(2 * c2, 2 * c2 + 2), slice(half * HALF, (half + 1) * HALF)
                    nc.vector.tensor_tensor(ctx_lo[:, part[0], part[1]], ctx_raw[:, half, part[0], :],
                                            ctx_hi[:, part[0], part[1]].bitcast(F32),
                                            ALU.subtract).then_inc(ctx_lo_done, 1)

            def row_stats(b, count):
                for i in range(b, b + count):
                    nc.vector.bn_stats(stats[:, i, :], y[:, i, :]).then_inc(stats_done, 1)

            def row_aggr(b, count, seen):
                for i in range(count):
                    dve.wait_ge(stats_done, seen + i + 1)
                    nc.vector.bn_aggr(mean_var[:, b + i, :], stats[:, b + i, :]).then_inc(aggr_done, 1)
                dve.wait_ge(aggr_done, seen + count)
                nc.vector.tensor_scalar(var_eps[:, b:b + count], mean_var[:, b:b + count, 1], EPS, None,
                                        ALU.add).then_inc(eps_added, 1)

            def row_norm(b, powers):
                dve.wait_ge(rstd_done, powers)
                nc.vector.tensor_scalar(norm_x[:, b % 2, :], y[:, b, :], mean_var[:, b, 0:1], rstd[:, b:b + 1],
                                        ALU.subtract, ALU.mult).then_inc(rows_normed, 1)

            def x_low(b):
                dve.wait_ge(xhi_stored, b + 1)
                cols = slice(b * P, (b + 1) * P)
                nc.vector.tensor_tensor(xn_lo[:, :, cols], out_ps[:, b % 2, :].rearrange("p (c n) -> p c n", c=C),
                                        xn_hi[:, :, cols].bitcast(F32), ALU.subtract).then_inc(xlo_stored, 1)

            def v_low(bank, p, n):
                dve.wait_ge(vhi_stored, B * p + n + 1)
                nc.vector.tensor_tensor(v_lo[:, n % B, :], job_ps[:, bank, 0:2 * P],
                                        v_hi[:, n % B, :].bitcast(F32), ALU.subtract).then_inc(vlo_stored, 1)

            def maxes(u, par):
                dve.wait_ge(scored, u + 1)
                nc.vector.tensor_reduce(neg_max[:, par, :], score_ps[:, par, :].rearrange("p (h m) -> p h m", h=H),
                                        AX_X, ALU.max, negate=True).then_inc(maxed, 1)

            def pt_low(t):
                dve.wait_ge(pthi_stored, t + 1)
                nc.vector.tensor_tensor(pt_lo[:, :], pt_ps[:, :], pt_hi[:, :].bitcast(F32),
                                        ALU.subtract).then_inc(ptlo_stored, 1)

            def normalise(u, par):
                dve.wait_ge(exped, u + 1)
                nc.vector.reciprocal(inv_sum[:, par, :], exp_sum[:, par, :]).then_inc(inverted, 1)
                dve.wait_ge(inverted, u + 1)
                nc.vector.tensor_tensor(prob[:, par, :, :], prob[:, par, :, :],
                                        inv_sum[:, par, :].unsqueeze(2).to_broadcast([P, H, P]),
                                        ALU.mult).then_inc(normed, 1)

            def ot_low(t, par, group):
                dve.wait_ge(othi_stored, t + 1)
                nc.vector.scalar_tensor_tensor(ot_lo[:, par, :], att_ps[:, :], bias_v[:, bass.ds(group, 1)],
                                               ot_hi[:, par, :].bitcast(F32), ALU.add,
                                               ALU.subtract).then_inc(otlo_stored, 1)

            def add_y(u, b, par):
                dve.wait_ge(projected, H * u + H)
                nc.vector.tensor_tensor(y[:, b, :], out_ps[:, par, :], y[:, b, :], ALU.add).then_inc(y_added, 1)

            plan = {}
            for n, (kind, index) in enumerate(PROLOGUE_JOBS):
                plan[(kind, index)] = n % 2
            ctx_low(0)
            dve.wait_ge(prior_logged, 1)
            nc.vector.tensor_tensor(gate_bias[:, :], out_ps[:, 0, E_ACT:2 * E_ACT], log_prior[:, :],
                                    ALU.add).then_inc(gate_bias_done, 1)
            dve.wait_ge(x_in[0], 16)
            row_stats(0, 4)
            row_aggr(0, 4, 0)
            v_low(plan[("v", 0)], 0, 0)
            row_norm(0, 1)
            v_low(plan[("v", 1)], 0, 1)
            row_norm(1, 1)
            ctx_low(1)
            v_low(plan[("v", 2)], 0, 2)
            v_low(plan[("v", 3)], 0, 3)
            for b in range(4):
                if b >= 2:
                    dve.wait_ge(rows_turned, b - 1)
                    row_norm(b, 1)
                if b >= 2:
                    x_low(b - 2)
            x_low(2)
            x_low(3)
            dve.wait_ge(x_in[1], 16)
            row_stats(4, 4)
            row_aggr(4, 4, 4)
            for b in range(4, 7):
                v_low(plan[("v", b)], 0, b)
            for b in range(4, 8):
                dve.wait_ge(rows_turned, b - 1)
                row_norm(b, 2)
                if b >= 6:
                    x_low(b - 2)
            x_low(6)
            x_low(7)
            maxes(0, 0)
            normalise(0, 0)
            maxes(1, 1)
            v_low(plan[("v", 7)], 0, 7)
            pt_low(0)
            normalise(1, 1)
            ot_low(0, 0, 0)
            dve.wait_ge(y_added, B)

            def x2_low(b):
                dve.wait_ge(x2hi_stored, b + 1)
                nc.vector.tensor_tensor(x2_lo[b % 2], x2_t[:, :, :], x2_hi[b % 2].bitcast(F32),
                                        ALU.subtract).then_inc(x2lo_stored, 1)

            def gate(b):
                z = job_ps[:, 0, 0:JR].rearrange("p (e r) -> p e r", e=E_ACT)
                dve.wait_ge(lora_in_done, b + 1)
                nc.vector.tensor_tensor(gates[:, 0, :], job_ps[:, 0, JR:JR + E_ACT], gate_bias[:, :],
                                        ALU.add).then_inc(gate_step, 1)
                dve.wait_ge(gate_step, 5 * b + 1)
                nc.vector.tensor_reduce(g_max[:, 0:1], gates[:, 0, :], AX_X, ALU.max, negate=True).then_inc(gate_step, 1)
                dve.wait_ge(gate_exped, b + 1)
                nc.vector.reciprocal(g_inv[:, 0:1], g_sum[:, 0:1]).then_inc(gate_step, 1)
                dve.wait_ge(gate_step, 5 * b + 3)
                nc.vector.tensor_scalar(gates[:, 2, :], gates[:, 1, :], g_inv[:, 0:1], LORA_SCALING, ALU.mult,
                                        ALU.mult).then_inc(gate_step, 1)
                dve.wait_ge(gate_step, 5 * b + 4)
                nc.vector.tensor_tensor(za[:, :, :], z, gates[:, 2, :].unsqueeze(2).to_broadcast([P, E_ACT, RANK]),
                                        ALU.mult).then_inc(gate_step, 1)

            def body(p, last):
                jobs = job_plan(last)
                for w in range(PU + (len(ENDING) if last else 0)):
                    u = PU * p + w
                    turn, mix = ffn_batches(u) if last else (None, None)
                    if mix is not None:
                        gate(mix)
                    if not (last and w + 2 >= PU):
                        maxes(u + 2, w % 2)
                    if not (last and w + 1 >= PU):
                        pt_low(u + 1)
                    if turn is not None:
                        if turn == 0:
                            dve.wait_ge(job_done["b"], 1)
                        if turn >= 2:
                            dve.wait_ge(rows_turned, B + turn - 1)
                        row_norm(turn, 2 + turn + 1)
                    if not (last and w + 2 >= PU):
                        normalise(u + 2, w % 2)
                    if not (last and w + 1 >= PU):
                        ot_low(u + 1, (w + 1) % 2, 2 * p + (w + 1) // B)
                    if turn is not None:
                        x2_low(turn)
                    if mix is not None:
                        dve.wait_ge(ffn_done, mix + 1)
                        nc.vector.tensor_tensor(y[:, mix, :], job_ps[:, 1, :], y[:, mix, :],
                                                ALU.add).then_inc(out_added, 1)
                    if w < PU:
                        add_y(u, w % B, w % 2)
                        for k, i in slot_jobs(w, last):
                            if k == "v":
                                v_low(jobs[(w, k, i)][0], p, i)
                        if last and w >= B:
                            dve.wait_ge(y_added, B + u + 1)
                            row_stats(w - B, 1)
                            row_aggr(w - B, 1, w)

            over_pairs(dve, body)

        @block.tensor
        def _(pe):
            def three(dst, terms):
                n = len(terms)
                for i, (s_hi, s_lo, m_hi, m_lo) in enumerate(terms):
                    nc.tensor.matmul(dst, s_hi, m_hi, start=(i == 0), stop=False)
                    nc.tensor.matmul(dst, s_hi, m_lo, start=False, stop=False)
                    ins = nc.tensor.matmul(dst, s_lo, m_hi, start=False, stop=(i == n - 1))
                return ins

            def job_q(bank, p, n):
                h, half = n % H, (n // H) % 2
                pe.wait_ge(lo_done["q"], 8 * p + H * (n // B) + h + 1)
                cols = slice(half * HALF, (half + 1) * HALF)
                three(job_ps[:, bank, :], [(wq_hi[:, h, c, :], wq_lo[:, h, c, :], xn_hi[:, c, cols],
                                            xn_lo[:, c, cols]) for c in range(C)]).then_inc(job_done["q"], 1)

            def job_k(bank, p, n):
                half = n % 2
                pe.wait_ge(lo_done["k"], 2 * p + n // 2 + 1)
                cols = slice(half * HALF, (half + 1) * HALF)
                three(job_ps[:, bank, :], [(wk_hi[:, c, :], wk_lo[:, c, :], ctx_hi[:, c, cols],
                                            ctx_lo[:, c, cols]) for c in range(C)]).then_inc(job_done["k"], 1)

            def job_v(bank, p, n):
                b = n % B
                pe.wait_ge(lo_done["v"], p + n // B + 1)
                cols = slice(b * P, (b + 1) * P)
                three(job_ps[:, bank, 0:2 * P], [(ctx_hi[:, c, cols], ctx_lo[:, c, cols], wv_hi[:, c, :],
                                                  wv_lo[:, c, :]) for c in range(C)]).then_inc(job_done["v"], 1)

            def job_a(bank, p, n):
                pe.wait_ge(ffn_in, 4 * 16)
                for c in range(C):
                    at = c * (JR + E_ACT)
                    cols = slice(c * P, (c + 1) * P)
                    nc.tensor.matmul(job_ps[:, bank, at:at + JR], la_raw[:, cols],
                                     sel_r[:, :, :].rearrange("p e r -> p (e r)"), start=True, stop=True)
                    ins = nc.tensor.matmul(job_ps[:, bank, at + JR:at + JR + E_ACT], rw_raw[:, cols], sel_e[:, :],
                                           start=True, stop=True)
                ins.then_inc(job_done["a"], 1)

            def job_b(bank, p, n):
                nc.tensor.matmul(job_ps[0:JR, bank, :], sel_r[:, :, :].rearrange("p e r -> p (e r)"), lb_raw,
                                 start=True, stop=True).then_inc(job_done["b"], 1)

            run_job = {"q": job_q, "k": job_k, "v": job_v, "a": job_a, "b": job_b}

            def scores(u, v, k_index):
                b, block4 = v % B, v // H
                pe.wait_ge(k_stored, k_index + 1)
                for h in range(H):
                    q = q_t[:, (H * block4 + h) % 8, (b % 4) * P:(b % 4 + 1) * P]
                    ins = nc.tensor.matmul(score_ps[:, v % 2, h * P:(h + 1) * P], q, k_t[:, b * P:(b + 1) * P],
                                           start=True, stop=True)
                ins.then_inc(scored, 1)

            def turn_probs(t, par):
                pe.wait_ge(normed, t + 1)
                for h in range(H):
                    ins = nc.tensor.transpose(pt_ps[:, h * P:(h + 1) * P], prob[:, par, h, :], ident[:, :])
                ins.then_inc(transposed, 1)

            def attend(t, v):
                b, odd = v % B, (v // B) % 2
                cols = slice(odd * P, (odd + 1) * P)
                pe.wait_ge(ptlo_stored, t + 1)
                three(att_ps[:, :], [(v_hi[:, b, cols], v_lo[:, b, cols], pt_hi[:, :], pt_lo[:, :])]
                      ).then_inc(attended, 1)

            def project(u, w):
                par = w % 2
                pe.wait_ge(otlo_stored, u + 1)
                for h in range(H):
                    cols = slice(h * P, (h + 1) * P)
                    for i, (s, m) in enumerate(((ot_hi, wo_hi), (ot_hi, wo_lo), (ot_lo, wo_hi))):
                        ins = nc.tensor.matmul(out_ps[:, par, :], s[:, par, cols], m[:, h, :],
                                               start=(h == 0 and i == 0), stop=(h == H - 1 and i == 2))
                    ins.then_inc(projected, 1)

            def turn_rows(b, dst):
                for c in range(C):
                    ins = nc.tensor.transpose(dst[:, c * P:(c + 1) * P], norm_x[:, b % 2, c * P:(c + 1) * P],
                                              ident[:, :])
                ins.then_inc(rows_turned, 1)

            pe.wait_ge(sel_step, 9)
            for i in range(2):
                ins = nc.tensor.matmul(out_ps[:, 0, i * E_ACT:(i + 1) * E_ACT], prior_rows[:, i, :], sel_e[:, :],
                                       start=True, stop=True)
            ins.then_inc(prior_picked, 1)

            before = {}
            for n, (kind, index) in enumerate(PROLOGUE_JOBS):
                before[(kind, index)] = (n % 2, PROLOGUE_JOBS[n - 2] if n >= 2 else None)

            def prologue_job(kind, index):
                bank, held = before[(kind, index)]
                if held:
                    s, count = stored(held[0], 0, held[1])
                    pe.wait_ge(s, count)
                run_job[kind](bank, 0, index)

            pe.wait_ge(ident_done, 1)
            pe.wait_ge(ctx_lo_done, 2)
            prologue_job("k", 0)
            for b in range(4):
                prologue_job("v", b)
            pe.wait_ge(gate_bias_done, 1)
            for b in range(4):
                pe.wait_ge(rows_normed, b + 1)
                if b >= 2:
                    pe.wait_ge(xlo_stored, b - 1)
                turn_rows(b, out_ps[:, b % 2, :])
            pe.wait_ge(ctx_lo_done, 4)
            for b in range(4, 7):
                prologue_job("v", b)
            pe.wait_ge(xlo_stored, 4)
            for j in range(4):
                prologue_job("q", j)
            for b in range(4, 8):
                pe.wait_ge(rows_normed, b + 1)
                pe.wait_ge(xlo_stored, b - 1)
                turn_rows(b, out_ps[:, b % 2, :])
            pe.wait_ge(q_stored, 4)
            scores(0, 0, 0)
            pe.wait_ge(xlo_stored, 8)
            prologue_job("q", 4)
            scores(1, 1, 0)
            prologue_job("v", 7)
            turn_probs(0, 0)
            prologue_job("q", 5)
            attend(0, 0)

            def turn_x2(b):
                pe.wait_ge(rows_normed, B + b + 1)
                if b:
                    pe.wait_ge(zat_stored, b)
                else:
                    for kind, index in (("q", UNITS - 1), ("k", 2 * G - 1), ("b", 0)):
                        s, count = stored(kind, 0, index)
                        pe.wait_ge(s, count)
                turn_rows(b, job_ps[:, 0, :])

            def lora_in(b):
                pe.wait_ge(x2lo_stored, b + 1)
                for c in range(C):
                    ins = nc.tensor.matmul(job_ps[:, 0, 0:JR + E_ACT], x2_t[:, c, :], az[:, c, :],
                                           start=(c == 0), stop=(c == C - 1))
                ins.then_inc(lora_in_done, 1)

            def base(b):
                pe.wait_ge(lo_done["o"], H * (G + 1))
                if b:
                    pe.wait_ge(out_added, b)
                for c in range(C):
                    for i, (s, m) in enumerate(((x2_hi, ctx_hi), (x2_hi, ctx_lo), (x2_lo, ctx_hi))):
                        nc.tensor.matmul(job_ps[:, 1, :], s[b % 2][:, c, :], m[:, c, 0:HID],
                                         start=(c == 0 and i == 0), stop=False)

            def turn_za(b):
                pe.wait_ge(gate_step, 5 * (b + 1))
                nc.tensor.matmul(job_ps[0:JR, 0, 0:P], za[:, :, :].rearrange("p e r -> p (e r)"), ident[:, :],
                                 start=True, stop=True).then_inc(za_turned, 1)

            def lora_out(b):
                pe.wait_ge(zat_stored, b + 1)
                nc.tensor.matmul(job_ps[:, 1, :], za_t[:, :], b_sel[:, :], start=False,
                                 stop=True).then_inc(ffn_done, 1)

            def body(p, last):
                jobs = job_plan(last)
                for w in range(PU + (len(ENDING) if last else 0)):
                    u = PU * p + w
                    turn, mix = ffn_batches(u) if last else (None, None)
                    if not (last and w + 2 >= PU):
                        pe.wait_ge(q_stored, PU * p + H * ((w + 2) // H) + H)
                        pe.wait_ge(exped, u + 1)
                        scores(u + 2, (w + 2) % PU, 4 * p + (w + 2) // H)
                    if not (last and w + 1 >= PU):
                        pe.wait_ge(ptlo_stored, u + 1)
                        turn_probs(u + 1, (w + 1) % 2)
                    if mix is not None:
                        base(mix)
                        turn_za(mix)
                    for kind, index in (slot_jobs(w, last) if w < PU else []):
                        if kind == "q":
                            bank, held = jobs[(w, kind, index)]
                            s, count = stored(held[0], p, held[1])
                            pe.wait_ge(s, count)
                            job_q(bank, p, index)
                    if not (last and w + 1 >= PU):
                        pe.wait_ge(vlo_stored, B * p + B * ((w + 1) // PU) + (w + 1) % B + 1)
                        pe.wait_ge(otlo_stored, u + 1)
                        attend(u + 1, (w + 1) % PU)
                    if mix is not None:
                        lora_out(mix)
                    if turn is not None:
                        turn_x2(turn)
                    if w < PU:
                        pe.wait_ge(lo_done["o"], 8 * p + H * (w // B) + H)
                        pe.wait_ge(y_added, B + u - 1)
                        project(u, w)
                        for kind, index in slot_jobs(w, last):
                            if kind != "q":
                                bank, held = jobs[(w, kind, index)]
                                s, count = stored(held[0], p, held[1])
                                pe.wait_ge(s, count)
                                run_job[kind](bank, p, index)
                    if turn is not None:
                        lora_in(turn)

            over_pairs(pe, body)


def kernel(**inputs):
    import numpy as np
    import concourse.bacc as bacc
    from concourse.bass_utils import run_bass_kernel_spmd

    a = {k: np.asarray(v) for k, v in inputs.items()}
    wkv, bkv = a["L0_xattn_Wkv"], a["L0_xattn_bkv"]
    kv = G * P

    def by_head(w, width):
        return w.reshape(C, P, -1, width).transpose(2, 1, 0, 3)

    laid = {
        "x": a["x"].transpose(1, 0, 2),
        "ctx_t": a["ctx_4096"].reshape(B * P, C, P).transpose(2, 1, 0),
        "wq": by_head(a["L0_xattn_Wq"], P),
        "wk": by_head(wkv[:, :kv], P),
        "wv": by_head(wkv[:, kv:], 2 * P),
        "wo": a["L0_xattn_Wo"].reshape(G * H, P, HID),
        "bq": a["L0_xattn_bq"].reshape(G * H, P).T,
        "bk": bkv[:kv].reshape(G, P).T,
        "bv": bkv[kv:].reshape(G, P).T,
        "bo": a["L0_xattn_bo"].reshape(1, HID),
        "w_base": a["L0_ffn_W_base"].T.reshape(C, P, HID),
        "b_base": a["L0_ffn_b_base"].reshape(1, HID),
        "lora_a": a["L0_ffn_lora_A"].reshape(ER, HID),
        "lora_b": a["L0_ffn_lora_B"].transpose(0, 2, 1).reshape(ER, HID),
        "router_w": a["L0_ffn_router_W"],
        "router_b": a["L0_ffn_router_b"].reshape(E_TOT, 1),
        "prior": a["L0_ffn_domain_prior"].reshape(E_TOT, 1),
        "active": a["L0_ffn_active"].reshape(1, E_ACT),
    }
    nc = bacc.Bacc("TRN2", target_bir_lowering=False, num_devices=1)
    arrays, args = {}, {}
    for name, arr in laid.items():
        arr = np.ascontiguousarray(arr)
        arrays[f"in_{name}"] = arr
        args[name] = nc.dram_tensor(f"in_{name}", arr.shape, mybir.dt.from_np(arr.dtype), kind="ExternalInput").ap()
    args["out"] = nc.dram_tensor("out_x", (B, P, HID), F32, kind="ExternalOutput").ap()
    build(nc, **args)
    r = run_bass_kernel_spmd(nc, [arrays], core_ids=[0])
    return r.results[0]["out_x"]
```

```python
from contextlib import ExitStack

import concourse.bass as bass
from concourse import mybir

F32 = mybir.dt.float32
F32R = mybir.dt.float32r
I32 = mybir.dt.int32
ALU = mybir.AluOpType
ACT = mybir.ActivationFunctionType
AX_X = mybir.AxisListType.X

P = 128
B = 8
HID = 512
C = HID // P
G = 8
H = 4
UNITS = G * B
PAIRS = G // 2
PU = 2 * B
HALF = B // 2 * P
E_TOT, E_ACT, RANK = 16, 4, 8
ER, JR = E_TOT * RANK, E_ACT * RANK
STACK = 3 * JR
SCALE = float(P) ** -0.5
EPS = 1e-5
PRIOR_EPS = 1e-12
LORA_SCALING = 16.0 / 8.0

PROLOGUE_JOBS = [("v", 0), ("v", 1), ("v", 2), ("v", 3), ("k", 0), ("v", 4), ("v", 5), ("v", 6),
                 ("q", 0), ("q", 1), ("q", 2), ("q", 3), ("q", 4), ("v", 7), ("q", 5)]
WARM_UP = 12
NORM_GROUPS = [(0, 2), (2, 2), (4, 4)]
KEY_SLOTS = {0: 1, 3: 2, 8: 3, 11: 4}
VALUE_SLOTS = {7 + b: b for b in range(B)}


def slot_jobs(w, last):
    jobs = []
    if not (last and w + 6 >= PU):
        jobs.append(("q", w + 6))
    if w in KEY_SLOTS and not (last and KEY_SLOTS[w] == 4):
        jobs.append(("k", KEY_SLOTS[w]))
    if w in VALUE_SLOTS and not last:
        jobs.append(("v", B + VALUE_SLOTS[w]))
    if last and w == 1:
        jobs.append(("a", 0))
    if last and w == 5:
        jobs.append(("b", 0))
    return jobs


PER_PAIR = {"q": PU, "k": 4, "v": B, "a": 0, "b": 0}


def job_plan(last):
    order = [(None, k, i) for k, i in PROLOGUE_JOBS]
    body = [(w, k, i) for w in range(PU) for k, i in slot_jobs(w, last)]
    plan, n = {}, len(order)
    before = [(k, i) for _, k, i in order[-2:]]
    for w, k, i in body:
        plan[(w, k, i)] = (n % 2, before[0])
        before = [before[1], (k, i)]
        n += 1
    return plan


def check_plan():
    body = [(k, i) for w in range(PU) for k, i in slot_jobs(w, False)]
    assert len(body) % 2 == 0
    assert [(k, i - PER_PAIR[k]) for k, i in body[-2:]] == PROLOGUE_JOBS[-2:]


def build(nc, x, ctx_t, wq, wk, wv, wo, bq, bk, bv, bo, w_base, b_base, lora_a, lora_b,
          router_w, router_b, prior, active, out):
    check_plan()
    stack = ExitStack()
    with stack:
        def sb(name, shape, dt=F32):
            return stack.enter_context(nc.sbuf_tensor(name, shape, dt))

        def ps(name, shape):
            return stack.enter_context(nc.psum_tensor(name, shape, F32))

        def sem(name):
            return stack.enter_context(nc.semaphore(name))

        xn_hi = sb("xn_hi", [P, C, B * P], F32R)
        xn_lo = sb("xn_lo", [P, C, B * P], F32R)
        ctx_hi = sb("ctx_hi", [P, C, B * P], F32R)
        ctx_lo = sb("ctx_lo", [P, C, B * P], F32R)
        wq_hi = sb("wq_hi", [P, H, C, P], F32R)
        wq_lo = sb("wq_lo", [P, H, C, P], F32R)
        wo_hi = sb("wo_hi", [P, H, HID], F32R)
        wo_lo = sb("wo_lo", [P, H, HID], F32R)
        wk_hi = sb("wk_hi", [P, C, P], F32R)
        wk_lo = sb("wk_lo", [P, C, P], F32R)
        wv_hi = sb("wv_hi", [P, C, 2 * P], F32R)
        wv_lo = sb("wv_lo", [P, C, 2 * P], F32R)
        raw_q = sb("raw_q", [P, 2, C, P])
        raw_o = sb("raw_o", [P, H, HID])
        raw_k = sb("raw_k", [P, C, P])
        raw_v = sb("raw_v", [P, C, 2 * P])
        k_t = sb("k_t", [P, B * P])
        v_hi = sb("v_hi", [P, B, 2 * P], F32R)
        v_lo = sb("v_lo", [P, B, 2 * P], F32R)
        q_t = sb("q_t", [P, 8, HALF])
        prob = sb("prob", [P, 2, H, P])
        pt_hi = sb("pt_hi", [P, H * P], F32R)
        pt_lo = sb("pt_lo", [P, H * P], F32R)
        ot_hi = sb("ot_hi", [P, 2, H * P], F32R)
        ot_lo = sb("ot_lo", [P, 2, H * P], F32R)
        y = sb("y", [P, B, HID])
        norm_x = sb("norm_x", [P, 2, HID])
        x2_t = sb("x2_t", [P, C, P])
        ident = sb("ident", [P, P])
        bias_q = sb("bias_q", [P, G * H])
        bias_k = sb("bias_k", [P, G])
        bias_v = sb("bias_v", [P, G])
        pair_q = sb("pair_q", [P, 3 * H])
        pair_k = sb("pair_k", [P, 3])
        pair_v = sb("pair_v", [P, 3])
        neg_max = sb("neg_max", [P, 2, H])
        exp_sum = sb("exp_sum", [P, 2, H])
        inv_sum = sb("inv_sum", [P, 2, H])
        stats = sb("stats", [P, B, 6])
        mean_var = sb("mean_var", [P, B, 2])
        var_eps = sb("var_eps", [P, B])
        rstd = sb("rstd", [P, B])
        minus_half = sb("minus_half", [P, B])
        prior_eps = sb("prior_eps", [P, 1])
        exp_ahead = sb("exp_ahead", [P, 1])
        ones = sb("ones", [P, P])
        act_i = sb("act_i", [P, E_ACT], I32)
        act_f = sb("act_f", [P, E_ACT])
        act_neg = sb("act_neg", [P, E_ACT])
        iota_i = sb("iota_i", [P, RANK], I32)
        iota_f = sb("iota_f", [P, RANK])
        sel_diff = sb("sel_diff", [P, E_ACT, RANK])
        sel_r = sb("sel_r", [P, 3, JR])
        sel_e = sb("sel_e", [E_TOT, E_ACT])
        prior_in = sb("prior_in", [E_TOT, 2])
        prior_rows = sb("prior_rows", [E_TOT, 2, P])
        log_prior = sb("log_prior", [P, E_ACT])
        gate_bias = sb("gate_bias", [P, E_ACT])
        az = sb("az", [P, C, JR + E_ACT])
        b_stack = sb("b_stack", [STACK, HID], F32R)
        gates = sb("gates", [P, 4, E_ACT])
        g_max, g_sum, g_inv = (sb(n, [P, 1]) for n in ("g_max", "g_sum", "g_inv"))
        za = sb("za", [P, 3, E_ACT, RANK])
        za_stack = sb("za_stack", [STACK, P], F32R)
        bo_all = x2_t[:, :, :].rearrange("p c n -> p (c n)")
        ctx_raw = q_t[:, :, :].rearrange("p a n -> p (a n)").rearrange("p (b c n) -> p b c n", b=B, c=C)
        lb_raw = norm_x[:, 0, :]
        base_all = raw_k[:, :, :].rearrange("p c n -> p (c n)")
        la_raw = raw_v[:, 0:2, :].rearrange("p c n -> p (c n)")
        rw_raw = raw_v[0:E_TOT, 2:4, :].rearrange("p c n -> p (c n)")
        x2_hi = [xn_hi[:, :, i * P:(i + 1) * P] for i in range(2)]
        x2_lo = [xn_lo[:, :, i * P:(i + 1) * P] for i in range(2)]

        score_ps = ps("score_ps", [P, 2, H * P])
        pt_ps = ps("pt_ps", [P, H * P])
        att_ps = ps("att_ps", [P, H * P])
        job_ps = ps("job_ps", [P, 2, HID])
        out_ps = ps("out_ps", [P, 2, HID])

        def ffn_ps(b):
            return job_ps[:, 1, :] if b < B - 1 else att_ps[:, :]

        small_in, ffn_in, bo_in, base_in = (sem(n) for n in ("small_in", "ffn_in", "bo_in", "base_in"))
        ctx_in = [sem(f"ctx_in{b}") for b in range(B)]
        x_in = [sem(f"x_in{i}") for i in range(len(NORM_GROUPS))]
        rawq_in = [sem(f"rawq_in{i}") for i in range(2)]
        rawo_in = [sem(f"rawo_in{i}") for i in range(H)]
        rawk_in, rawv_in = sem("rawk_in"), sem("rawv_in")
        rawv_first = [sem(f"rawv_first{i}") for i in range(2)]
        ctx_hi_done = sem("ctx_hi_done")
        ctx_lo_early, ctx_lo_late = sem("ctx_lo_early"), sem("ctx_lo_late")
        wv_first = sem("wv_first")
        hi_done = {k: sem(f"w{k}_hi_done") for k in "qokv"}
        wv_lo_first = [sem(f"wv_lo_first{i}") for i in range(2)]
        lo_done = {k: sem(f"w{k}_lo_done") for k in "qokv"}
        job_done = {k: sem(f"job_{k}_done") for k in "qkvab"}
        q_stored, k_stored = sem("q_stored"), sem("k_stored")
        vhi_stored, vlo_stored = sem("vhi_stored"), sem("vlo_stored")
        az_stored, bsel_stored = sem("az_stored"), sem("bsel_stored")
        scored, maxed, exped, inverted, normed = (sem(n) for n in (
            "scored", "maxed", "exped", "inverted", "normed"))
        transposed, pthi_stored, ptlo_stored = sem("transposed"), sem("pthi_stored"), sem("ptlo_stored")
        attended, othi_stored, otlo_stored = sem("attended"), sem("othi_stored"), sem("otlo_stored")
        projected, y_added = sem("projected"), sem("y_added")
        biases_picked = sem("biases_picked")
        const_done, ident_done, sel_step, bias_done = (sem(n) for n in (
            "const_done", "ident_done", "sel_step", "bias_done"))
        prior_picked, prior_logged, gate_bias_done = (sem(n) for n in (
            "prior_picked", "prior_logged", "gate_bias_done"))
        stats_done, aggr_done, eps_added, rstd_done, rows_normed = (sem(n) for n in (
            "stats_done", "aggr_done", "eps_added", "rstd_done", "rows_normed"))
        rows_turned, xhi_stored, xlo_stored = sem("rows_turned"), sem("xhi_stored"), sem("xlo_stored")
        x2t_stored, x2hi_stored, x2lo_stored = sem("x2t_stored"), sem("x2hi_stored"), sem("x2lo_stored")
        lora_in_done, gate_step, gate_exped = sem("lora_in_done"), sem("gate_step"), sem("gate_exped")
        za_turned, zat_stored = sem("za_turned"), sem("zat_stored")
        base_added, bsel_hi, za_hi = sem("base_added"), sem("bsel_hi"), sem("za_hi")
        ffn_done, out_added, out_stored = sem("ffn_done"), sem("out_added"), sem("out_stored")

        block = stack.enter_context(nc.Block())

        def stored(kind, p, index):
            s = {"q": q_stored, "k": k_stored, "v": vlo_stored, "a": az_stored, "b": bsel_stored}
            return s[kind], PER_PAIR[kind] * p + index + 1

        def over_pairs(eng, body):
            with eng.Fori(0, PAIRS - 1, 1) as p:
                body(p, False)
            body(PAIRS - 1, True)

        def ffn_batches(u):
            turn, mix = u - (UNITS - B + 1), u - (UNITS - B + 2)
            return (turn if 0 <= turn < B else None), (mix if 0 <= mix < B else None)

        ENDING = range(UNITS, UNITS + 2)

        @block.sync
        def _(sp):
            def load_q(p, n):
                s = n % 2
                sp.dma_start(raw_q[:, s, :, :], wq[PU // 2 * p + n, :, :, :]).then_inc(rawq_in[s], 16)

            def load_ctx(b):
                sp.dma_start(ctx_raw[:, b, :, :], ctx_t[b, :, :, :]).then_inc(ctx_in[b], 16)

            def load_x(i):
                b, count = NORM_GROUPS[i]
                sp.dma_start(y[:, b:b + count, :], x[:, b:b + count, :]).then_inc(x_in[i], 16)

            def load_first_v(i):
                sp.dma_start(raw_v[:, 2 * i:2 * i + 2, :], wv[0, :, 2 * i:2 * i + 2, :]).then_inc(rawv_first[i], 16)

            load_first_v(0)
            load_ctx(0)
            load_first_v(1)
            for b in range(1, 4):
                load_ctx(b)
            sp.dma_start(raw_k[:, :, :], wk[0, :, :, :]).then_inc(rawk_in, 16)
            sp.dma_start(act_i[:, :], active.to_broadcast([P, E_ACT])).then_inc(small_in, 16)
            sp.dma_start(prior_in[:, 0:1], prior).then_inc(small_in, 16)
            sp.dma_start(prior_in[:, 1:2], router_b).then_inc(small_in, 16)
            sp.dma_start(bias_q[:, :], bq).then_inc(small_in, 16)
            sp.dma_start(bias_k[:, :], bk).then_inc(small_in, 16)
            sp.dma_start(bias_v[:, :], bv).then_inc(small_in, 16)
            load_x(0)
            load_ctx(4)
            load_ctx(5)
            load_x(1)
            load_q(0, 0)
            load_q(0, 1)
            load_ctx(6)
            load_ctx(7)
            sp.dma_start(bo_all, bo.to_broadcast([P, HID])).then_inc(bo_in, 16)
            load_x(2)
            for n in range(2, H):
                sp.wait_ge(lo_done["q"], n - 1)
                load_q(0, n)
            for h in range(H):
                sp.dma_start(raw_o[:, h, :], wo[h, :, :]).then_inc(rawo_in[h], 16)

            def loads(p, last):
                if last:
                    sp.wait_ge(rows_turned, B)
                    sp.wait_ge(lo_done["v"], PAIRS - 1)
                    sp.dma_start(lb_raw, lora_b).then_inc(ffn_in, 16)
                    sp.dma_start(la_raw, lora_a).then_inc(ffn_in, 16)
                    sp.dma_start(rw_raw, router_w).then_inc(ffn_in, 16)
                for odd in range(2):
                    if not (last and odd):
                        for h in range(H):
                            n = H * (odd + 1) + h
                            sp.wait_ge(lo_done["q"], 8 * p + n - 1)
                            load_q(p, n)
                            if h == 1:
                                sp.wait_ge(lo_done["k"], 2 * p + odd + 1)
                                sp.dma_start(raw_k[:, :, :], wk[2 * p + odd + 1, :, :, :]).then_inc(rawk_in, 16)
                        if odd == 0 and not last:
                            sp.wait_ge(job_done["v"], B * (p + 1))
                            sp.dma_start(raw_v[:, :, :], wv[p + 1, :, :, :]).then_inc(rawv_in, 16)
                    for h in range(H):
                        sp.wait_ge(lo_done["o"], 8 * p + H * odd + h + 1)
                        if last and odd:
                            sp.dma_start(raw_o[:, h, :], w_base[h, :, :]).then_inc(rawo_in[h], 16)
                        else:
                            sp.dma_start(raw_o[:, h, :], wo[8 * p + H * (odd + 1) + h, :, :]).then_inc(rawo_in[h], 16)

            over_pairs(sp, loads)
            sp.wait_ge(lo_done["k"], G)
            sp.dma_start(base_all, b_base.to_broadcast([P, HID])).then_inc(base_in, 16)
            for b in range(B):
                sp.wait_ge(out_added, b + 1)
                sp.dma_start(out[b, :, :], y[:, b, :]).then_inc(out_stored, 16)
            sp.wait_ge(out_stored, 16 * B)

        @block.gpsimd
        def _(pool):
            nc.gpsimd.memset(ident[:, :], 0.0).then_inc(const_done, 1)
            nc.gpsimd.memset(ones[:, :], 1.0).then_inc(const_done, 1)
            nc.gpsimd.memset(minus_half[:, :], -0.5).then_inc(const_done, 1)
            nc.gpsimd.memset(prior_eps[:, :], PRIOR_EPS).then_inc(const_done, 1)
            nc.gpsimd.iota(iota_i[:, :], pattern=[[1, RANK]], base=0, channel_multiplier=-1).then_inc(const_done, 1)
            pool.wait_ge(const_done, 5)
            nc.gpsimd.affine_select(out=ident[:, :], in_=ident[:, :], compare_op=ALU.not_equal, fill=1.0,
                                    base=0, pattern=[[-1, P]], channel_multiplier=1).then_inc(ident_done, 1)

            def low(kind, p, n, dst, raw, hi):
                pool.wait_ge(hi_done[kind], p + n + 1)
                nc.gpsimd.tensor_tensor(dst, raw, hi.bitcast(F32), ALU.subtract).then_inc(lo_done[kind], 1)

            def low_q(p, n):
                h = n % H
                low("q", 8 * p, n, wq_lo[:, h, :, :], raw_q[:, n % 2, :, :], wq_hi[:, h, :, :])

            def low_o(p, n):
                h = n % H
                low("o", 8 * p, n, wo_lo[:, h, :], raw_o[:, h, :], wo_hi[:, h, :])

            def low_k(p, n):
                low("k", 2 * p, n, wk_lo[:, :, :], raw_k[:, :, :], wk_hi[:, :, :])

            def low_v(p, n):
                low("v", p - 1, n, wv_lo[:, :, :], raw_v[:, :, :], wv_hi[:, :, :])

            def power(first, count):
                nc.gpsimd.tensor_tensor(rstd[:, first:first + count], var_eps[:, first:first + count],
                                        minus_half[:, 0:count], ALU.pow).then_inc(rstd_done, 1)

            def ctx_low(b):
                pool.wait_ge(ctx_hi_done, b + 1)
                cols = slice(b * P, (b + 1) * P)
                nc.gpsimd.tensor_tensor(ctx_lo[:, :, cols], ctx_raw[:, b, :, :], ctx_hi[:, :, cols].bitcast(F32),
                                        ALU.subtract).then_inc(ctx_lo_late, 1)

            def first_power(i):
                pool.wait_ge(eps_added, i + 1)
                power(*NORM_GROUPS[i])

            def add_bo(b):
                pool.wait_ge(rows_normed, b + 1)
                nc.gpsimd.tensor_tensor(y[:, b, :], y[:, b, :], bo_all, ALU.add).then_inc(y_added, 1)

            low_k(0, 0)
            first_power(0)
            ctx_low(4)
            ctx_low(5)
            first_power(1)
            ctx_low(6)
            low_q(0, 0)
            ctx_low(7)
            low_q(0, 1)
            first_power(2)
            low_q(0, 2)
            low_q(0, 3)
            pool.wait_ge(bo_in, 16)
            for b in range(4):
                add_bo(b)
            for n in range(H):
                low_o(0, n)
            for b in range(4, 8):
                add_bo(b)

            def add_base(b):
                if b == 0:
                    pool.wait_ge(base_in, 16)
                pool.wait_ge(rows_normed, B + b + 1)
                nc.gpsimd.tensor_tensor(y[:, b, :], y[:, b, :], base_all, ALU.add).then_inc(base_added, 1)

            def lows(p, last):
                for w in range(PU):
                    odd, wg = divmod(w, B)
                    if wg < H and not (last and odd):
                        low_q(p, H * (odd + 1) + wg)
                        if wg == 1:
                            low_k(p, odd + 1)
                    if w == 4 and not last:
                        low_v(p, 1)
                    if wg == 7 and not (last and odd):
                        for h in range(H):
                            low_o(p, H * (odd + 1) + h)
                    if last and odd:
                        if wg == 1:
                            for c in range(C):
                                pool.wait_ge(hi_done["o"], H * G + c + 1)
                                nc.gpsimd.tensor_tensor(ctx_lo[:, c, 0:HID], raw_o[:, c, :],
                                                        ctx_hi[:, c, 0:HID].bitcast(F32),
                                                        ALU.subtract).then_inc(lo_done["o"], 1)
                        if wg:
                            add_base(wg - 1)
                        pool.wait_ge(eps_added, len(NORM_GROUPS) + wg + 1)
                        power(wg, 1)
                if last:
                    add_base(B - 1)

            over_pairs(pool, lows)

        @block.scalar
        def _(act):
            def high(kind, dst, raw):
                nc.scalar.activation(dst, raw, ACT.Copy).then_inc(hi_done[kind], 1)

            def high_q(p, n, first=False):
                h = n % H
                act.wait_ge(rawq_in[n % 2], 16 * (4 * p + n // 2 + 1))
                if not first:
                    act.wait_ge(job_done["q"], PU * p + B * (n // H - 1) + H + h + 1)
                high("q", wq_hi[:, h, :, :], raw_q[:, n % 2, :, :])

            def high_o(p, n, first=False):
                h = n % H
                act.wait_ge(rawo_in[h], 16 * (2 * p + n // H + 1))
                if not first:
                    act.wait_ge(projected, H * PU * p + H * B * (n // H) - H + h + 1)
                high("o", wo_hi[:, h, :], raw_o[:, h, :])

            def high_k(p, n, first=False):
                act.wait_ge(rawk_in, 16 * (2 * p + n + 1))
                if not first:
                    act.wait_ge(job_done["k"], 4 * p + 2 * n)
                high("k", wk_hi[:, :, :], raw_k[:, :, :])

            def high_v(p, n):
                act.wait_ge(rawv_in, 16 * (p + n))
                act.wait_ge(job_done["v"], B * (p + n))
                high("v", wv_hi[:, :, :], raw_v[:, :, :])

            def pick_biases(p, groups, picked):
                nc.scalar.copy(pair_q[:, 0:H * groups], bias_q[:, bass.ds(8 * p, H * groups)]).then_inc(biases_picked, 1)
                nc.scalar.copy(pair_k[:, 0:groups], bias_k[:, bass.ds(2 * p, groups)]).then_inc(biases_picked, 1)
                nc.scalar.copy(pair_v[:, 0:groups], bias_v[:, bass.ds(2 * p, groups)]).then_inc(biases_picked, 1)
                act.wait_ge(biases_picked, picked)

            def store_q(bank, p, n):
                act.wait_ge(job_done["q"], PU * p + n + 1)
                head = H * (n // B) + n % H
                nc.scalar.activation(q_t[:, n % 8, :], job_ps[:, bank, :], ACT.Identity,
                                     bias=pair_q[:, head:head + 1], scale=SCALE).then_inc(q_stored, 1)

            def store_k(bank, p, n):
                half = n % 2
                act.wait_ge(job_done["k"], 4 * p + n + 1)
                nc.scalar.activation(k_t[:, half * HALF:(half + 1) * HALF], job_ps[:, bank, :], ACT.Identity,
                                     bias=pair_k[:, n // 2:n // 2 + 1]).then_inc(k_stored, 1)

            def store_v(bank, p, n):
                act.wait_ge(job_done["v"], B * p + n + 1)
                nc.scalar.activation(v_hi[:, n % B, :], job_ps[:, bank, 0:2 * P], ACT.Copy).then_inc(vhi_stored, 1)

            def store_az(bank):
                act.wait_ge(job_done["a"], 1)
                nc.scalar.activation(az[:, :, :], job_ps[:, bank, 0:C * (JR + E_ACT)].rearrange(
                    "p (c n) -> p c n", c=C), ACT.Copy).then_inc(az_stored, 1)

            def store_bsel(bank):
                act.wait_ge(job_done["b"], 1)
                nc.scalar.activation(b_stack[:, :], job_ps[0:STACK, bank, :], ACT.Copy).then_inc(bsel_hi, 1)

            def exps(u, par):
                act.wait_ge(maxed, u + 1)
                for h in range(H):
                    last = nc.scalar.activation(prob[:, par, h, :], score_ps[:, par, h * P:(h + 1) * P], ACT.Exp,
                                                bias=neg_max[:, par, h:h + 1],
                                                accum_out=exp_sum[:, par, h:h + 1])
                last.then_inc(exped, 1)

            def store_pt(t):
                act.wait_ge(transposed, t + 1)
                nc.scalar.activation(pt_hi[:, :], pt_ps[:, :], ACT.Copy).then_inc(pthi_stored, 1)

            def store_ot(t, par, group):
                act.wait_ge(attended, t + 1)
                nc.scalar.activation(ot_hi[:, par, :], att_ps[:, :], ACT.Identity,
                                     bias=pair_v[:, group:group + 1]).then_inc(othi_stored, 1)

            def store_x(b):
                act.wait_ge(rows_turned, b + 1)
                nc.scalar.activation(xn_hi[:, :, b * P:(b + 1) * P],
                                     out_ps[:, b % 2, :].rearrange("p (c n) -> p c n", c=C),
                                     ACT.Copy).then_inc(xhi_stored, 1)

            def split_ctx(b):
                act.wait_ge(ctx_in[b], 16)
                nc.scalar.activation(ctx_hi[:, :, b * P:(b + 1) * P], ctx_raw[:, b, :, :],
                                     ACT.Copy).then_inc(ctx_hi_done, 1)

            bank = {job: n % 2 for n, job in enumerate(PROLOGUE_JOBS)}

            def first_store(kind, index):
                {"q": store_q, "k": store_k, "v": store_v}[kind](bank[(kind, index)], 0, index)

            split_ctx(0)
            for c2 in range(0, C, 2):
                act.wait_ge(rawv_first[c2 // 2], 16)
                nc.scalar.activation(wv_hi[:, c2:c2 + 2, :], raw_v[:, c2:c2 + 2, :], ACT.Copy).then_inc(wv_first, 1)
            for b in range(1, 4):
                split_ctx(b)
            high_k(0, 0, True)
            first_store("v", 0)
            first_store("v", 1)
            split_ctx(4)
            first_store("v", 2)
            split_ctx(5)
            first_store("v", 3)
            act.wait_ge(bias_done, 1)
            pick_biases(0, 3, 3)
            high_q(0, 0, True)
            split_ctx(6)
            first_store("k", 0)
            store_x(0)
            store_x(1)
            first_store("v", 4)
            high_q(0, 1, True)
            split_ctx(7)
            first_store("v", 5)
            store_x(2)
            store_x(3)
            first_store("v", 6)
            high_q(0, 2, True)
            first_store("q", 0)
            high_q(0, 3, True)
            first_store("q", 1)
            high_o(0, 0, True)
            store_x(4)
            store_x(5)
            act.wait_ge(prior_picked, 1)
            nc.scalar.activation(log_prior[:, :], att_ps[:, 0:E_ACT], ACT.Ln,
                                 bias=prior_eps[:, 0:1]).then_inc(prior_logged, 1)
            nc.scalar.activation(exp_ahead[:, :], prior_eps[:, :], ACT.Exp)
            high_o(0, 1, True)
            first_store("q", 2)
            store_x(6)
            first_store("q", 3)
            store_x(7)
            high_o(0, 2, True)
            high_o(0, 3, True)
            exps(0, 0)
            first_store("q", 4)
            exps(1, 1)
            store_pt(0)
            first_store("v", 7)
            first_store("q", 5)
            store_ot(0, 0, 0)

            def turn_x2(b):
                act.wait_ge(rows_turned, B + b + 1)
                src = job_ps[:, 0, :].rearrange("p (c n) -> p c n", c=C)
                nc.scalar.activation(x2_t[:, :, :], src, ACT.Copy).then_inc(x2t_stored, 1)
                nc.scalar.activation(x2_hi[b % 2], src, ACT.Copy).then_inc(x2hi_stored, 1)

            def gate_exp(b):
                act.wait_ge(gate_step, 5 * b + 2)
                nc.scalar.activation(gates[:, 1, :], gates[:, 0, :], ACT.Exp, bias=g_max[:, 0:1],
                                     accum_out=g_sum[:, 0:1]).then_inc(gate_exped, 1)

            def store_zat(b, par):
                act.wait_ge(za_turned, b + 1)
                nc.scalar.activation(za_stack[:, :], out_ps[0:STACK, par, 0:P], ACT.Copy).then_inc(za_hi, 1)

            def body(p, last):
                jobs = job_plan(last)
                act.wait_ge(q_stored, PU * p + 6)
                act.wait_ge(k_stored, 4 * p + 1)
                act.wait_ge(othi_stored, PU * p + 1)
                pick_biases(p, 2 if last else 3, 3 * p + 6)
                for w in range(PU + (len(ENDING) if last else 0)):
                    u = PU * p + w
                    odd, wg = divmod(w, B)
                    turn, mix = ffn_batches(u) if last else (None, None)
                    if not (last and w + 1 >= PU):
                        store_pt(u + 1)
                    if not (last and w + 2 >= PU):
                        exps(u + 2, w % 2)
                    if mix is not None:
                        store_zat(mix, w % 2)
                    if wg < H and not (last and odd):
                        high_q(p, H * (odd + 1) + wg)
                        if wg == 1:
                            high_k(p, odd + 1)
                    if w == 4 and not last:
                        high_v(p, 1)
                    mine = [(k, i) for k, i in (slot_jobs(w, last) if w < PU else [])]
                    for k, i in mine:
                        if k == "q":
                            store_q(jobs[(w, k, i)][0], p, i)
                    if not (last and w + 1 >= PU):
                        store_ot(u + 1, (w + 1) % 2, (w + 1) // B)
                    if wg == 7 and w < PU and not (last and odd):
                        for h in range(H):
                            high_o(p, H * (odd + 1) + h)
                    if turn is not None:
                        turn_x2(turn)
                    for k, i in mine:
                        if k == "k":
                            store_k(jobs[(w, k, i)][0], p, i)
                        if k == "v":
                            store_v(jobs[(w, k, i)][0], p, i)
                        if k == "a":
                            store_az(jobs[(w, k, i)][0])
                        if k == "b":
                            store_bsel(jobs[(w, k, i)][0])
                    if turn is not None:
                        gate_exp(turn)
                    if last and w == B:
                        act.wait_ge(job_done["k"], 2 * G)
                        act.wait_ge(job_done["v"], PAIRS * B)
                        for c in range(C):
                            act.wait_ge(rawo_in[c], 16 * (G + 1))
                            nc.scalar.activation(ctx_hi[:, c, 0:HID], raw_o[:, c, :],
                                                 ACT.Copy).then_inc(hi_done["o"], 1)

            over_pairs(act, body)

        @block.vector
        def _(dve):
            def scale_bias():
                dve.wait_ge(small_in, 6 * 16)
                nc.vector.tensor_scalar(bias_q[:, :], bias_q[:, :], SCALE, None, ALU.mult).then_inc(bias_done, 1)

            def selectors():
                nc.vector.tensor_copy(act_f[:, :], act_i[:, :]).then_inc(sel_step, 1)
                dve.wait_ge(const_done, 5)
                nc.vector.tensor_copy(iota_f[:, :], iota_i[:, :]).then_inc(bias_done, 1)
                for i in range(2):
                    nc.vector.tensor_scalar(prior_rows[:, i, :], ones[0:E_TOT, :], prior_in[:, i:i + 1], None,
                                            ALU.mult).then_inc(sel_step, 1)
                dve.wait_ge(sel_step, 3)
                nc.vector.tensor_scalar(act_neg[:, :], act_f[:, :], 0.0, float(E_TOT), ALU.is_lt,
                                        ALU.mult).then_inc(sel_step, 1)
                dve.wait_ge(sel_step, 4)
                nc.vector.tensor_tensor(act_f[:, :], act_f[:, :], act_neg[:, :], ALU.add).then_inc(sel_step, 1)
                dve.wait_ge(sel_step, 5)
                nc.vector.tensor_scalar(act_f[:, :], act_f[:, :], float(E_TOT - 1), 0.0, ALU.min,
                                        ALU.max).then_inc(sel_step, 1)
                dve.wait_ge(sel_step, 6)
                dve.wait_ge(bias_done, 2)
                nc.vector.tensor_scalar(sel_e[:, :], act_f[0:E_TOT, :], iota_f[0:E_TOT, 0:1], 0.0, ALU.add,
                                        ALU.is_equal).then_inc(sel_step, 1)
                nc.vector.scalar_tensor_tensor(
                    sel_diff[:, :, :], act_f[:, :].unsqueeze(2).to_broadcast([P, E_ACT, RANK]), float(RANK),
                    iota_f[:, :].unsqueeze(1).to_broadcast([P, E_ACT, RANK]), ALU.mult, ALU.add).then_inc(sel_step, 1)
                dve.wait_ge(sel_step, 8)
                nc.vector.tensor_scalar(
                    sel_r[:, :, :], sel_diff[:, :, :].rearrange("p e r -> p (e r)").unsqueeze(1).to_broadcast(
                        [P, 3, JR]), 0.0, None, ALU.is_equal).then_inc(sel_step, 1)

            def ctx_low(b):
                dve.wait_ge(ctx_hi_done, b + 1)
                cols = slice(b * P, (b + 1) * P)
                nc.vector.tensor_tensor(ctx_lo[:, :, cols], ctx_raw[:, b, :, :], ctx_hi[:, :, cols].bitcast(F32),
                                        ALU.subtract).then_inc(ctx_lo_early, 1)

            def row_stats(b, count):
                for i in range(b, b + count):
                    nc.vector.bn_stats(stats[:, i, :], y[:, i, :]).then_inc(stats_done, 1)

            def row_aggr(b, count, seen):
                for i in range(count):
                    dve.wait_ge(stats_done, seen + i + 1)
                    nc.vector.bn_aggr(mean_var[:, b + i, :], stats[:, b + i, :]).then_inc(aggr_done, 1)
                dve.wait_ge(aggr_done, seen + count)
                nc.vector.tensor_scalar(var_eps[:, b:b + count], mean_var[:, b:b + count, 1], EPS, None,
                                        ALU.add).then_inc(eps_added, 1)

            def row_norm(b, powers):
                dve.wait_ge(rstd_done, powers)
                nc.vector.tensor_scalar(norm_x[:, b % 2, :], y[:, b, :], mean_var[:, b, 0:1], rstd[:, b:b + 1],
                                        ALU.subtract, ALU.mult).then_inc(rows_normed, 1)

            def x_low(b):
                dve.wait_ge(xhi_stored, b + 1)
                cols = slice(b * P, (b + 1) * P)
                nc.vector.tensor_tensor(xn_lo[:, :, cols], out_ps[:, b % 2, :].rearrange("p (c n) -> p c n", c=C),
                                        xn_hi[:, :, cols].bitcast(F32), ALU.subtract).then_inc(xlo_stored, 1)

            def v_low(bank, p, n):
                dve.wait_ge(vhi_stored, B * p + n + 1)
                nc.vector.tensor_tensor(v_lo[:, n % B, :], job_ps[:, bank, 0:2 * P],
                                        v_hi[:, n % B, :].bitcast(F32), ALU.subtract).then_inc(vlo_stored, 1)

            def maxes(u, par):
                dve.wait_ge(scored, u + 1)
                nc.vector.tensor_reduce(neg_max[:, par, :], score_ps[:, par, :].rearrange("p (h m) -> p h m", h=H),
                                        AX_X, ALU.max, negate=True).then_inc(maxed, 1)

            def pt_low(t):
                dve.wait_ge(pthi_stored, t + 1)
                nc.vector.tensor_tensor(pt_lo[:, :], pt_ps[:, :], pt_hi[:, :].bitcast(F32),
                                        ALU.subtract).then_inc(ptlo_stored, 1)

            def normalise(u, par):
                dve.wait_ge(exped, u + 1)
                nc.vector.reciprocal(inv_sum[:, par, :], exp_sum[:, par, :]).then_inc(inverted, 1)
                dve.wait_ge(inverted, u + 1)
                nc.vector.tensor_tensor(prob[:, par, :, :], prob[:, par, :, :],
                                        inv_sum[:, par, :].unsqueeze(2).to_broadcast([P, H, P]),
                                        ALU.mult).then_inc(normed, 1)

            def ot_low(t, par, group):
                dve.wait_ge(othi_stored, t + 1)
                nc.vector.scalar_tensor_tensor(ot_lo[:, par, :], att_ps[:, :], bias_v[:, bass.ds(group, 1)],
                                               ot_hi[:, par, :].bitcast(F32), ALU.add,
                                               ALU.subtract).then_inc(otlo_stored, 1)

            def add_y(u, b, par):
                dve.wait_ge(projected, H * u + H)
                nc.vector.tensor_tensor(y[:, b, :], out_ps[:, par, :], y[:, b, :], ALU.add).then_inc(y_added, 1)

            bank = {job: n % 2 for n, job in enumerate(PROLOGUE_JOBS)}

            def first_v_low(b):
                v_low(bank[("v", b)], 0, b)

            def norm_group(i):
                b, count = NORM_GROUPS[i]
                dve.wait_ge(x_in[i], 16)
                row_stats(b, count)
                row_aggr(b, count, b)

            def first_norm(b):
                if b >= 2:
                    dve.wait_ge(rows_turned, b - 1)
                row_norm(b, 1 if b < 2 else 2 if b < 4 else 3)

            ctx_low(0)
            for c in range(0, C, 2):
                dve.wait_ge(wv_first, c // 2 + 1)
                nc.vector.tensor_tensor(wv_lo[:, c:c + 2, :], raw_v[:, c:c + 2, :],
                                        wv_hi[:, c:c + 2, :].bitcast(F32), ALU.subtract).then_inc(wv_lo_first[c // 2], 1)
            for b in range(1, 4):
                ctx_low(b)
            first_v_low(0)
            first_v_low(1)
            norm_group(0)
            first_v_low(2)
            first_norm(0)
            first_norm(1)
            scale_bias()
            norm_group(1)
            first_v_low(3)
            first_norm(2)
            first_norm(3)
            x_low(0)
            x_low(1)
            first_v_low(4)
            first_v_low(5)
            x_low(2)
            x_low(3)
            dve.wait_ge(x_in[2], 16)
            row_stats(4, 2)
            first_v_low(6)
            row_stats(6, 2)
            row_aggr(4, 4, 4)
            selectors()
            first_norm(4)
            first_norm(5)
            x_low(4)
            first_norm(6)
            x_low(5)
            first_norm(7)
            dve.wait_ge(prior_logged, 1)
            nc.vector.tensor_tensor(gate_bias[:, :], att_ps[:, E_ACT:2 * E_ACT], log_prior[:, :],
                                    ALU.add).then_inc(gate_bias_done, 1)
            x_low(6)
            x_low(7)
            maxes(0, 0)
            normalise(0, 0)
            maxes(1, 1)
            pt_low(0)
            normalise(1, 1)
            first_v_low(7)
            ot_low(0, 0, 0)
            dve.wait_ge(y_added, B)

            def x2_low(b):
                dve.wait_ge(x2hi_stored, b + 1)
                nc.vector.tensor_tensor(x2_lo[b % 2], x2_t[:, :, :], x2_hi[b % 2].bitcast(F32),
                                        ALU.subtract).then_inc(x2lo_stored, 1)

            def gate_logits(b, par):
                dve.wait_ge(lora_in_done, b + 1)
                nc.vector.tensor_tensor(gates[:, 0, :], out_ps[:, par, JR:JR + E_ACT], gate_bias[:, :],
                                        ALU.add).then_inc(gate_step, 1)
                dve.wait_ge(gate_step, 5 * b + 1)
                nc.vector.tensor_reduce(g_max[:, 0:1], gates[:, 0, :], AX_X, ALU.max, negate=True).then_inc(gate_step, 1)

            def gate_inputs(b, par):
                dve.wait_ge(gate_exped, b + 1)
                nc.vector.reciprocal(g_inv[:, 0:1], g_sum[:, 0:1]).then_inc(gate_step, 1)
                dve.wait_ge(gate_step, 5 * b + 3)
                nc.vector.tensor_scalar(gates[:, 2, :], gates[:, 1, :], g_inv[:, 0:1], LORA_SCALING, ALU.mult,
                                        ALU.mult).then_inc(gate_step, 1)
                dve.wait_ge(gate_step, 5 * b + 4)
                z = out_ps[:, par, 0:JR].unsqueeze(1).to_broadcast([P, 3, JR]).rearrange(
                    "p s (e r) -> p s e r", e=E_ACT)
                alpha = gates[:, 2, :].unsqueeze(1).unsqueeze(3).to_broadcast([P, 3, E_ACT, RANK])
                nc.vector.tensor_tensor(za[:, :, :, :], z, alpha, ALU.mult).then_inc(gate_step, 1)

            def stack_low(dst, src, rows, hi_done_, count, done):
                dve.wait_ge(hi_done_, count)
                nc.vector.tensor_tensor(dst[rows, :], src, dst[rows, :].bitcast(F32), ALU.subtract).then_inc(done, 1)

            def za_low(b, par):
                rows = slice(2 * JR, 3 * JR)
                stack_low(za_stack, out_ps[rows, par, 0:P], rows, za_hi, b + 1, zat_stored)

            def b_low(bank):
                rows = slice(JR, 2 * JR)
                stack_low(b_stack, job_ps[rows, bank, :], rows, bsel_hi, 1, bsel_stored)

            def body(p, last):
                jobs = job_plan(last)
                for w in range(PU + (len(ENDING) if last else 0)):
                    u = PU * p + w
                    turn, mix = ffn_batches(u) if last else (None, None)
                    if not (last and w + 2 >= PU):
                        maxes(u + 2, w % 2)
                    if not (last and w + 1 >= PU):
                        pt_low(u + 1)
                    if mix is not None:
                        za_low(mix, w % 2)
                    if turn is not None:
                        if turn == 0:
                            dve.wait_ge(job_done["b"], 1)
                        if turn >= 2:
                            dve.wait_ge(rows_turned, B + turn - 1)
                        if w < PU:
                            row_norm(turn, len(NORM_GROUPS) + turn + 1)
                    if not (last and w + 2 >= PU):
                        normalise(u + 2, w % 2)
                    if not (last and w + 1 >= PU):
                        ot_low(u + 1, (w + 1) % 2, 2 * p + (w + 1) // B)
                    if mix is not None:
                        dve.wait_ge(ffn_done, mix + 1)
                        dve.wait_ge(base_added, mix + 1)
                        nc.vector.tensor_tensor(y[:, mix, :], ffn_ps(mix), y[:, mix, :],
                                                ALU.add).then_inc(out_added, 1)
                    if turn is not None and w < PU:
                        x2_low(turn)
                    if w < PU:
                        add_y(u, w % B, w % 2)
                        for k, i in slot_jobs(w, last):
                            if k == "v":
                                v_low(jobs[(w, k, i)][0], p, i)
                            if k == "b":
                                b_low(jobs[(w, k, i)][0])
                    if turn is not None:
                        gate_logits(turn, (w + 1) % 2)
                    if last and B <= w < PU:
                        dve.wait_ge(y_added, B + u + 1)
                        row_stats(w - B, 1)
                        if w < PU - 1 and turn is not None:
                            gate_inputs(turn, (w + 1) % 2)
                        row_aggr(w - B, 1, w)
                        if w == PU - 1:
                            gate_inputs(turn, (w + 1) % 2)
                            row_norm(B - 1, len(NORM_GROUPS) + B)
                    elif turn is not None:
                        if w >= PU:
                            x2_low(turn)
                        gate_inputs(turn, (w + 1) % 2)

            over_pairs(dve, body)

        @block.tensor
        def _(pe):
            def three(dst, terms):
                n = len(terms)
                for i, (s_hi, s_lo, m_hi, m_lo) in enumerate(terms):
                    nc.tensor.matmul(dst, s_hi, m_hi, start=(i == 0), stop=False)
                    nc.tensor.matmul(dst, s_hi, m_lo, start=False, stop=False)
                    ins = nc.tensor.matmul(dst, s_lo, m_hi, start=False, stop=(i == n - 1))
                return ins

            def job_q(bank, p, n):
                h, half = n % H, (n // H) % 2
                pe.wait_ge(lo_done["q"], 8 * p + H * (n // B) + h + 1)
                cols = slice(half * HALF, (half + 1) * HALF)
                three(job_ps[:, bank, :], [(wq_hi[:, h, c, :], wq_lo[:, h, c, :], xn_hi[:, c, cols],
                                            xn_lo[:, c, cols]) for c in range(C)]).then_inc(job_done["q"], 1)

            def job_k(bank, p, n):
                half = n % 2
                pe.wait_ge(lo_done["k"], 2 * p + n // 2 + 1)
                cols = slice(half * HALF, (half + 1) * HALF)
                three(job_ps[:, bank, :], [(wk_hi[:, c, :], wk_lo[:, c, :], ctx_hi[:, c, cols],
                                            ctx_lo[:, c, cols]) for c in range(C)]).then_inc(job_done["k"], 1)

            def job_v(bank, p, n):
                b = n % B
                if n >= B:
                    pe.wait_ge(lo_done["v"], p + n // B)
                cols = slice(b * P, (b + 1) * P)
                three(job_ps[:, bank, 0:2 * P], [(ctx_hi[:, c, cols], ctx_lo[:, c, cols], wv_hi[:, c, :],
                                                  wv_lo[:, c, :]) for c in range(C)]).then_inc(job_done["v"], 1)

            def job_a(bank, p, n):
                pe.wait_ge(ffn_in, 3 * 16)
                for c in range(C):
                    at = c * (JR + E_ACT)
                    cols = slice(c * P, (c + 1) * P)
                    nc.tensor.matmul(job_ps[:, bank, at:at + JR], la_raw[:, cols],
                                     sel_r[:, 0, :], start=True, stop=True)
                    ins = nc.tensor.matmul(job_ps[:, bank, at + JR:at + JR + E_ACT], rw_raw[:, cols], sel_e[:, :],
                                           start=True, stop=True)
                ins.then_inc(job_done["a"], 1)

            def job_b(bank, p, n):
                nc.tensor.matmul(job_ps[0:STACK, bank, :], sel_r[:, :, :].rearrange("p s n -> p (s n)"), lb_raw,
                                 start=True, stop=True).then_inc(job_done["b"], 1)

            run_job = {"q": job_q, "k": job_k, "v": job_v, "a": job_a, "b": job_b}

            def scores(u, v, k_index):
                b, block4 = v % B, v // H
                pe.wait_ge(k_stored, k_index + 1)
                for h in range(H):
                    q = q_t[:, (H * block4 + h) % 8, (b % 4) * P:(b % 4 + 1) * P]
                    ins = nc.tensor.matmul(score_ps[:, v % 2, h * P:(h + 1) * P], q, k_t[:, b * P:(b + 1) * P],
                                           start=True, stop=True)
                ins.then_inc(scored, 1)

            def turn_probs(t, par):
                pe.wait_ge(normed, t + 1)
                for h in range(H):
                    ins = nc.tensor.transpose(pt_ps[:, h * P:(h + 1) * P], prob[:, par, h, :], ident[:, :])
                ins.then_inc(transposed, 1)

            def attend(t, v):
                b, odd = v % B, (v // B) % 2
                cols = slice(odd * P, (odd + 1) * P)
                pe.wait_ge(ptlo_stored, t + 1)
                three(att_ps[:, :], [(v_hi[:, b, cols], v_lo[:, b, cols], pt_hi[:, :], pt_lo[:, :])]
                      ).then_inc(attended, 1)

            def project(u, w, p):
                par = w % 2
                pe.wait_ge(otlo_stored, u + 1)
                for h in range(H):
                    if h == 0 or w % B == 0:
                        pe.wait_ge(lo_done["o"], 8 * p + H * (w // B) + (h + 1 if w % B == 0 else H))
                    cols = slice(h * P, (h + 1) * P)
                    for i, (s, m) in enumerate(((ot_hi, wo_hi), (ot_hi, wo_lo), (ot_lo, wo_hi))):
                        ins = nc.tensor.matmul(out_ps[:, par, :], s[:, par, cols], m[:, h, :],
                                               start=(h == 0 and i == 0), stop=(h == H - 1 and i == 2))
                    ins.then_inc(projected, 1)

            def turn_rows(b, dst):
                for c in range(C):
                    ins = nc.tensor.transpose(dst[:, c * P:(c + 1) * P], norm_x[:, b % 2, c * P:(c + 1) * P],
                                              ident[:, :])
                ins.then_inc(rows_turned, 1)

            held = {job: (n % 2, PROLOGUE_JOBS[n - 2] if n >= 2 else None) for n, job in enumerate(PROLOGUE_JOBS)}

            def first_job(kind, index):
                bank, before = held[(kind, index)]
                if before:
                    s, count = stored(before[0], 0, before[1])
                    pe.wait_ge(s, count)
                run_job[kind](bank, 0, index)

            def first_turn(b):
                pe.wait_ge(rows_normed, b + 1)
                if b >= 2:
                    pe.wait_ge(xlo_stored, b - 1)
                turn_rows(b, out_ps[:, b % 2, :])

            pe.wait_ge(ident_done, 1)
            for _ in range(WARM_UP):
                nc.tensor.matmul(score_ps[:, 0, 0:P], ident[:, :], ident[:, :], start=True, stop=True)
            for c in range(2):
                pe.wait_ge(wv_lo_first[c], 1)
            for b in range(4):
                pe.wait_ge(ctx_lo_early, b + 1)
                first_job("v", b)
            first_job("k", 0)
            first_turn(0)
            first_turn(1)
            for b in range(4, 6):
                pe.wait_ge(ctx_lo_late, b - 3)
                first_job("v", b)
            first_turn(2)
            first_turn(3)
            pe.wait_ge(ctx_lo_late, 3)
            first_job("v", 6)
            pe.wait_ge(xlo_stored, 4)
            first_job("q", 0)
            first_job("q", 1)
            first_turn(4)
            first_turn(5)
            pe.wait_ge(sel_step, 9)
            for i in range(2):
                ins = nc.tensor.matmul(att_ps[:, i * E_ACT:(i + 1) * E_ACT], prior_rows[:, i, :], sel_e[:, :],
                                       start=True, stop=True)
            ins.then_inc(prior_picked, 1)
            first_job("q", 2)
            first_turn(6)
            first_job("q", 3)
            first_turn(7)
            pe.wait_ge(q_stored, 4)
            scores(0, 0, 0)
            scores(1, 1, 0)
            pe.wait_ge(xlo_stored, 8)
            first_job("q", 4)
            pe.wait_ge(ctx_lo_late, 4)
            first_job("v", 7)
            turn_probs(0, 0)
            first_job("q", 5)
            pe.wait_ge(gate_bias_done, 1)
            attend(0, 0)

            def turn_x2(b):
                pe.wait_ge(rows_normed, B + b + 1)
                if b:
                    pe.wait_ge(x2lo_stored, b)
                else:
                    for kind, index in (("q", UNITS - 1), ("k", 2 * G - 1), ("b", 0)):
                        s, count = stored(kind, 0, index)
                        pe.wait_ge(s, count)
                turn_rows(b, job_ps[:, 0, :])

            def lora_in(b, par):
                pe.wait_ge(x2t_stored, b + 1)
                pe.wait_ge(y_added, UNITS + b + 1)
                pe.wait_ge(az_stored, 1)
                for c in range(C):
                    ins = nc.tensor.matmul(out_ps[:, par, 0:JR + E_ACT], x2_t[:, c, :], az[:, c, :],
                                           start=(c == 0), stop=(c == C - 1))
                ins.then_inc(lora_in_done, 1)

            def turn_za(b, par):
                pe.wait_ge(gate_step, 5 * (b + 1))
                nc.tensor.matmul(out_ps[0:STACK, par, 0:P], za[:, :, :, :].rearrange("p s e r -> p (s e r)"), ident[:, :],
                                 start=True, stop=True).then_inc(za_turned, 1)

            def base_high(b):
                pe.wait_ge(lo_done["o"], H * (G + 1))
                if 0 < b < B - 1:
                    pe.wait_ge(out_added, b)
                if b == B - 1:
                    pe.wait_ge(otlo_stored, UNITS)
                pe.wait_ge(x2hi_stored, b + 1)
                for c in range(C):
                    for m in (ctx_hi, ctx_lo):
                        nc.tensor.matmul(ffn_ps(b), x2_hi[b % 2][:, c, :], m[:, c, 0:HID],
                                         start=(c == 0 and m is ctx_hi), stop=False)

            def base_low(b):
                pe.wait_ge(x2lo_stored, b + 1)
                for c in range(C):
                    nc.tensor.matmul(ffn_ps(b), x2_lo[b % 2][:, c, :], ctx_hi[:, c, 0:HID],
                                     start=False, stop=False)

            def lora_out(b):
                pe.wait_ge(zat_stored, b + 1)
                pe.wait_ge(bsel_stored, 1)
                nc.tensor.matmul(ffn_ps(b), za_stack[:, :], b_stack[:, :], start=False,
                                 stop=True).then_inc(ffn_done, 1)

            def body(p, last):
                jobs = job_plan(last)
                for w in range(PU + (len(ENDING) if last else 0)):
                    u = PU * p + w
                    turn, mix = ffn_batches(u) if last else (None, None)
                    if not (last and w + 2 >= PU):
                        pe.wait_ge(q_stored, PU * p + H * ((w + 2) // H) + H)
                        pe.wait_ge(exped, u + 1)
                        scores(u + 2, (w + 2) % PU, 4 * p + (w + 2) // H)
                    if not (last and w + 1 >= PU):
                        pe.wait_ge(ptlo_stored, u + 1)
                        turn_probs(u + 1, (w + 1) % 2)
                    if mix is not None:
                        base_high(mix)
                        turn_za(mix, w % 2)
                        if turn is not None and w >= PU:
                            turn_x2(turn)
                        base_low(mix)
                    for kind, index in (slot_jobs(w, last) if w < PU else []):
                        if kind == "q":
                            bank, held = jobs[(w, kind, index)]
                            s, count = stored(held[0], p, held[1])
                            pe.wait_ge(s, count)
                            job_q(bank, p, index)
                    if not (last and w + 1 >= PU):
                        pe.wait_ge(vlo_stored, B * p + B * ((w + 1) // PU) + (w + 1) % B + 1)
                        pe.wait_ge(otlo_stored, u + 1)
                        attend(u + 1, (w + 1) % PU)
                    if mix is not None:
                        lora_out(mix)
                    if turn is not None and w < PU:
                        turn_x2(turn)
                    if w < PU:
                        pe.wait_ge(y_added, B + u - 1)
                        project(u, w, p)
                        for kind, index in slot_jobs(w, last):
                            if kind != "q":
                                bank, held = jobs[(w, kind, index)]
                                s, count = stored(held[0], p, held[1])
                                pe.wait_ge(s, count)
                                run_job[kind](bank, p, index)
                    if turn is not None:
                        lora_in(turn, (w + 1) % 2)

            over_pairs(pe, body)


def kernel(**inputs):
    import numpy as np
    import concourse.bacc as bacc
    from concourse.bass_utils import run_bass_kernel_spmd

    a = {k: np.asarray(v) for k, v in inputs.items()}
    wkv, bkv = a["L0_xattn_Wkv"], a["L0_xattn_bkv"]
    kv = G * P

    def by_head(w, width):
        return w.reshape(C, P, -1, width).transpose(2, 1, 0, 3)

    laid = {
        "x": a["x"].transpose(1, 0, 2),
        "ctx_t": a["ctx_4096"].reshape(B, P, C, P).transpose(0, 3, 2, 1),
        "wq": by_head(a["L0_xattn_Wq"], P),
        "wk": by_head(wkv[:, :kv], P),
        "wv": by_head(wkv[:, kv:], 2 * P),
        "wo": a["L0_xattn_Wo"].reshape(G * H, P, HID),
        "bq": a["L0_xattn_bq"].reshape(G * H, P).T,
        "bk": bkv[:kv].reshape(G, P).T,
        "bv": bkv[kv:].reshape(G, P).T,
        "bo": a["L0_xattn_bo"].reshape(1, HID),
        "w_base": a["L0_ffn_W_base"].T.reshape(C, P, HID),
        "b_base": a["L0_ffn_b_base"].reshape(1, HID),
        "lora_a": a["L0_ffn_lora_A"].reshape(ER, HID),
        "lora_b": a["L0_ffn_lora_B"].transpose(0, 2, 1).reshape(ER, HID),
        "router_w": a["L0_ffn_router_W"],
        "router_b": a["L0_ffn_router_b"].reshape(E_TOT, 1),
        "prior": a["L0_ffn_domain_prior"].reshape(E_TOT, 1),
        "active": a["L0_ffn_active"].reshape(1, E_ACT),
    }
    nc = bacc.Bacc("TRN2", target_bir_lowering=False, num_devices=1)
    arrays, args = {}, {}
    for name, arr in laid.items():
        arr = np.ascontiguousarray(arr)
        arrays[f"in_{name}"] = arr
        args[name] = nc.dram_tensor(f"in_{name}", arr.shape, mybir.dt.from_np(arr.dtype), kind="ExternalInput").ap()
    args["out"] = nc.dram_tensor("out_x", (B, P, HID), F32, kind="ExternalOutput").ap()
    build(nc, **args)
    r = run_bass_kernel_spmd(nc, [arrays], core_ids=[0])
    return r.results[0]["out_x"]
```
